# Optimizing a Trainium2 kernel written in Bass

```python
import numpy as np
import jax
import jax.numpy as jnp

def _softmax(x, axis=-1):
    return jax.nn.softmax(x, axis=axis)

def _gelu(x):
    return jax.nn.gelu(x, approximate=True)

def _silu(x):
    return jax.nn.silu(x)

def _sigmoid(x):
    return jax.nn.sigmoid(x)

def _layernorm(x, axis=-1, eps=1e-05):
    m = jnp.mean(x, axis=axis, keepdims=True)
    v = jnp.var(x, axis=axis, keepdims=True)
    return (x - m) / jnp.sqrt(v + eps)

def _scatter_add(tgt, idx, src, axis=0):
    return tgt.at[idx].add(src)

def _segment_sum(src, seg, n):
    return jax.ops.segment_sum(src, seg, n)
kernel_name = 'mk_gnn_resnorm_d1_gnn_r32_82b123'

def setup_inputs(seed: int=0):
    np.random.seed(seed)
    _w = jnp.asarray

    def _rec_inputs():
        import jax
        import jax.numpy as jnp
        _gk = jax.random.key(seed)
        x = -1.686e-05 + 1 * jax.random.normal(jax.random.fold_in(_gk, 1), (50000, 160), jnp.float32)
        src = jax.random.randint(jax.random.fold_in(_gk, 2), (50000,), 0, 50000, jnp.int32)
        dst = jnp.minimum((50000 * jax.random.uniform(jax.random.fold_in(_gk, 3), (50000,)) ** 2.0).astype(jnp.int32), 49999)
        _o = jnp.argsort(dst, stable=True)
        src = src[_o]
        dst = dst[_o]
        edge_attr_4 = -0.000107899 + 1.00008 * jax.random.normal(jax.random.fold_in(_gk, 12), (50000, 4), jnp.float32)
        edge_attr_8 = 0.000398945 + 1.00003 * jax.random.normal(jax.random.fold_in(_gk, 13), (50000, 8), jnp.float32)
        node_vec1 = jax.random.uniform(jax.random.fold_in(_gk, 14), (50000, 1), jnp.float32, 0.0, 1)
        return (x, src, dst, edge_attr_4, edge_attr_8, node_vec1)
    x, src, dst, edge_attr_4, edge_attr_8, node_vec1 = _rec_inputs()

    def _L0_gnn_setup():
        import jax, jax.numpy as jnp
        import numpy as np
        INV3 = 1.0 / np.sqrt(3.0)

        def _fctp(x_s, x_v, attr, w0, w1):
            s = x_s @ w0 * (1.0 / np.sqrt(x_s.shape[-1])) * attr
            v = jnp.einsum('nud,uw->nwd', x_v, w1) * (1.0 / np.sqrt(x_v.shape[-2])) * attr[..., None]
            return (s, v)
        key = jax.random.key(seed)
        ks = jax.random.split(key, 16)
        N, E = (50000, 25000)
        inp = {'node_input': jax.random.normal(ks[0], (N, 160), jnp.float32), 'node_attr': jnp.ones((N, 1), jnp.float32), 'edge_attr': jax.random.normal(ks[1], (E, 4), jnp.float32), 'edge_scalars': jax.random.normal(ks[2], (E, 8), jnp.float32), 'sc_w0': jax.random.normal(ks[3], (64, 64), jnp.float32), 'sc_w1': jax.random.normal(ks[4], (32, 32), jnp.float32), 'lin1_w0': jax.random.normal(ks[5], (64, 64), jnp.float32), 'lin1_w1': jax.random.normal(ks[6], (32, 32), jnp.float32), 'fc_w1': jax.random.normal(ks[7], (8, 64), jnp.float32), 'fc_w2': jax.random.normal(ks[8], (64, 192), jnp.float32), 'lin2_w0': jax.random.normal(ks[9], (96, 64), jnp.float32), 'lin2_w1': jax.random.normal(ks[10], (96, 32), jnp.float32), 'lin3_w': jax.random.normal(ks[11], (96, 1), jnp.float32), 'edge_src': jax.random.randint(ks[12], (E,), 0, N), 'edge_dst': jax.random.randint(ks[13], (E,), 0, N), 'num_neighbors': 16}
        return inp
    _L0_gnn_all = _L0_gnn_setup()
    _L0_gnn_in = {k: v for k, v in _L0_gnn_all.items() if k in ('sc_w0', 'sc_w1', 'lin1_w0', 'lin1_w1', 'fc_w1', 'fc_w2', 'lin2_w0', 'lin2_w1', 'lin3_w')}
    del _L0_gnn_all
    return {'x': x, 'src': src, 'dst': dst, 'edge_attr_4': edge_attr_4, 'edge_attr_8': edge_attr_8, 'node_vec1': node_vec1, 'L0_gnn_sc_w0': _L0_gnn_in['sc_w0'], 'L0_gnn_sc_w1': _L0_gnn_in['sc_w1'], 'L0_gnn_lin1_w0': _L0_gnn_in['lin1_w0'], 'L0_gnn_lin1_w1': _L0_gnn_in['lin1_w1'], 'L0_gnn_fc_w1': _L0_gnn_in['fc_w1'], 'L0_gnn_fc_w2': _L0_gnn_in['fc_w2'], 'L0_gnn_lin2_w0': _L0_gnn_in['lin2_w0'], 'L0_gnn_lin2_w1': _L0_gnn_in['lin2_w1'], 'L0_gnn_lin3_w': _L0_gnn_in['lin3_w']}

def reference(x, src, dst, edge_attr_4, edge_attr_8, node_vec1, L0_gnn_sc_w0, L0_gnn_sc_w1, L0_gnn_lin1_w0, L0_gnn_lin1_w1, L0_gnn_fc_w1, L0_gnn_fc_w2, L0_gnn_lin2_w0, L0_gnn_lin2_w1, L0_gnn_lin3_w):
    import jax
    import jax.numpy as jnp

    def _L0_gnn_ref(node_input, node_attr, edge_attr, edge_scalars, sc_w0, sc_w1, lin1_w0, lin1_w1, fc_w1, fc_w2, lin2_w0, lin2_w1, lin3_w, edge_src, edge_dst, num_neighbors):
        import jax, jax.numpy as jnp
        import numpy as np
        INV3 = 1.0 / np.sqrt(3.0)

        def _fctp(x_s, x_v, attr, w0, w1):
            s = x_s @ w0 * (1.0 / np.sqrt(x_s.shape[-1])) * attr
            v = jnp.einsum('nud,uw->nwd', x_v, w1) * (1.0 / np.sqrt(x_v.shape[-2])) * attr[..., None]
            return (s, v)
        N = node_input.shape[0]
        h = jax.nn.silu(edge_scalars @ fc_w1 * (1.0 / np.sqrt(8.0)))
        weight = h @ fc_w2 * (1.0 / np.sqrt(64.0))
        xs, xv = (node_input[:, :64], node_input[:, 64:].reshape(N, 32, 3))
        sc_s, sc_v = _fctp(xs, xv, node_attr, sc_w0, sc_w1)
        f_s, f_v = _fctp(xs, xv, node_attr, lin1_w0, lin1_w1)
        gs = f_s[edge_src]
        gv = f_v[edge_src]
        ys, yv = (edge_attr[:, :1], edge_attr[:, 1:])
        w1_, w2_ = (weight[:, :64], weight[:, 64:128])
        w3_, w4_ = (weight[:, 128:160], weight[:, 160:192])
        m0a = gs * ys * w1_
        m0b = jnp.sum(gv * yv[:, None, :], -1) * INV3 * w4_
        m1a = gs[..., None] * yv[:, None, :] * w2_[..., None]
        m1b = gv * ys[..., None] * w3_[..., None]
        E = m0a.shape[0]
        edge_feat = jnp.concatenate([m0a, m0b, m1a.reshape(E, 192), m1b.reshape(E, 96)], -1)
        mid = jax.ops.segment_sum(edge_feat, edge_dst, num_segments=N)
        mid = mid / np.sqrt(float(num_neighbors))
        mid_s, mid_v = (mid[:, :96], mid[:, 96:].reshape(N, 96, 3))
        c_s, c_v = _fctp(mid_s, mid_v, node_attr, lin2_w0, lin2_w1)
        conv = jnp.concatenate([c_s, c_v.reshape(N, -1)], -1)
        scfeat = jnp.concatenate([sc_s, sc_v.reshape(N, -1)], -1)
        angle = 0.1 * (mid_s @ lin3_w) * (1.0 / np.sqrt(96.0)) * node_attr
        return jnp.cos(angle) * scfeat + jnp.sin(angle) * conv
    x = _layernorm(x + _L0_gnn_ref(x, node_vec1, edge_attr_4, edge_attr_8, L0_gnn_sc_w0, L0_gnn_sc_w1, L0_gnn_lin1_w0, L0_gnn_lin1_w1, L0_gnn_fc_w1, L0_gnn_fc_w2, L0_gnn_lin2_w0, L0_gnn_lin2_w1, L0_gnn_lin3_w, src, dst, 16), axis=-1)
    return x

_drawn_inputs = setup_inputs


def setup_inputs(seed=0):
    import zlib

    import numpy as np

    out = dict(_drawn_inputs(seed))
    spreads = {}
    factors = {'edge_attr_4': 8.0,
     'edge_attr_8': 8.0,
     'L0_gnn_lin1_w0': 8.0,
     'L0_gnn_lin1_w1': 8.0,
     'L0_gnn_fc_w1': 8.0,
     'L0_gnn_fc_w2': 8.0,
     'L0_gnn_lin2_w0': 8.0,
     'L0_gnn_lin2_w1': 8.0,
     'L0_gnn_lin3_w': 8.0}
    for name, (base, spread) in spreads.items():
        noise = np.random.default_rng([zlib.crc32(name.encode()), seed]).standard_normal(out[name].shape)
        drawn = base * np.exp(spread * noise) if base else spread * noise
        out[name] = jnp.asarray(drawn.astype(out[name].dtype))
    for name, factor in factors.items():
        out[name] = (out[name] * factor).astype(out[name].dtype)
    return out
```

```python
import concourse.bass as bass
from concourse import mybir
from contextlib import ExitStack
import math
import numpy as np

P = 128
NS, NV, MU = 64, 96, 32
ROW = NS + NV
ROWA = ROW + 1
NW = 2 * NS + 2 * MU
OUTW = ROWA + MU
G = 4
EPS = 1e-5
NEIGHBORS = 16.0


UNROLL = 4


class Step:

    def __init__(self, i, c):
        self.i, self.c = i, c
        self.n = c if i is None else i * UNROLL + c

    def __add__(self, d):
        return Step(self.i, self.c + d)

    def slot(self, slots=2):
        return self.c % slots

    def round(self, slots=2):
        return self.c // slots if self.i is None else self.i * (UNROLL // slots) + self.c // slots

    def within(self, count):
        return self.i is not None or 0 <= self.c < count


def wait(eng, sem, count):
    if not isinstance(count, int) or count > 0:
        eng.wait_ge(sem, count)


def software_pipeline(eng, first, last, fill, drain, step):
    count = max(drain - fill + 1, 0) // UNROLL
    for k in range(first, fill):
        step(Step(None, k))
    if count:
        with eng.Fori(0, count, 1) as i:
            for u in range(UNROLL):
                step(Step(i, fill + u))
    for k in range(fill + UNROLL * count, last + 1):
        step(Step(None, k))


def gnn_program(nc, xa, src, dst, dst_rows, ea4, ea8t, fc_w1, fc_w2, lin1_s, lin1_v, lin2_a, lin2_b,
                sc_s, sc_v, ident, later, acc0, acc1, out):
    fp32, i32 = mybir.dt.float32, mybir.dt.int32
    ALU, ACT = mybir.AluOpType, mybir.ActivationFunctionType
    NT = dst.shape[1]
    NPAIR = NT // 2
    NG = NT // G
    NODES = NT * P
    xa_g = xa.rearrange("(g p j) c -> g p (j c)", p=P, j=G)
    out_g = out.rearrange("(g p j) c -> g p (j c)", p=P, j=G)
    accs = [acc0, acc1]
    acc_g = [a[0:NODES, :].rearrange("(g p j) c -> g p (j c)", p=P, j=G) for a in accs]

    with ExitStack() as ctx:
        def sb(name, shape, dt=fp32):
            return ctx.enter_context(nc.sbuf_tensor(name, shape, dt))

        def ps(name):
            return ctx.enter_context(nc.psum_tensor(name, [P, 512], fp32))

        def sem(name):
            return ctx.enter_context(nc.semaphore(name))

        ident_sb = sb("ident_sb", [P, P])
        later_sb = sb("later_sb", [P, P])
        fc_w1_sb = sb("fc_w1_sb", [8, NS])
        fc_w2_sb = sb("fc_w2_sb", [P, NW])
        lin1_s_sb = sb("lin1_s_sb", [P, NS])
        lin1_v_sb = sb("lin1_v_sb", [NV, NV])
        lin2_a_sb = sb("lin2_a_sb", [P, NS + 1 + MU])
        lin2_b_sb = sb("lin2_b_sb", [P, OUTW])
        sc_s_sb = sb("sc_s_sb", [P, NS])
        sc_v_sb = sb("sc_v_sb", [NV, NV])
        half_pi = sb("half_pi", [P, 1])
        minus_half = sb("minus_half", [P, G])
        dst_i = sb("dst_i", [P, NT], i32)
        dst_f = sb("dst_f", [P, NT])
        spare_row = sb("spare_row", [P, NT], i32)
        to_spare = sb("to_spare", [P, NT])
        ea4_sb = sb("ea4_sb", [P, NT, 4])
        zeros = sb("zeros", [P, 3 * ROWA])
        src_sb = sb("src_sb", [P, UNROLL, 2], i32)
        x_sb = sb("x_sb", [P, UNROLL, 2, ROWA])
        e8_sb = sb("e8_sb", [8, UNROLL, 2 * P])
        dstrow_sb = sb("dstrow_sb", [P, UNROLL, 2, P], i32)
        xt_sb = sb("xt_sb", [P, 2, 4 * P])
        h_sb = sb("h_sb", [P, 2, P])
        f_sb = sb("f_sb", [P, 2, 2, ROW])
        q_sb = sb("q_sb", [P, 2, 2, 4])
        tm_sb = sb("tm_sb", [P, 2, 3, MU])
        ts_sb = sb("ts_sb", [P, 2, MU])
        pa_sb = sb("pa_sb", [P, 2, 2, P])
        pb_sb = sb("pb_sb", [P, 2, 2, P])
        pt_sb = sb("pt_sb", [P, 2, 4 * P])
        vq_sb = sb("vq_sb", [P, 2, MU, 3])
        feat_sb = sb("feat_sb", [P, 2, 2, OUTW])
        same_sb = sb("same_sb", [P, 2, 2, P])
        junk_sb = sb("junk_sb", [P, 2, P])
        later_cnt = sb("later_cnt", [P, 2, 2])
        shift_sb = sb("shift_sb", [P, 2, 2])
        row_sb = sb("row_sb", [P, UNROLL, 2], i32)
        comb_sb = sb("comb_sb", [P, UNROLL, 2, ROWA])
        xn_sb = sb("xn_sb", [P, 2, G, ROWA])
        c0_sb = sb("c0_sb", [P, 2, G, ROWA])
        c1_sb = sb("c1_sb", [P, 2, G, ROWA])
        cs_sb = sb("cs_sb", [P, 2, G, ROWA])
        xnt_sb = sb("xnt_sb", [P, 2, 2, 4 * P])
        y_sb = sb("y_sb", [P, 2, G, ROW])
        ang = sb("ang", [P, G])
        turns = sb("turns", [P, G])
        red = sb("red", [P, 2, G])
        redabs = sb("redabs", [P, G])
        trig = sb("trig", [P, 2, 2, G])
        trig_a = sb("trig_a", [P, 2, G])
        stats = sb("stats", [P, G, 6])
        meanvar = sb("meanvar", [P, 2, G, 2])
        vareps = sb("vareps", [P, G])
        rstd = sb("rstd", [P, 2, G])
        XT, Z, F, PT, OUT, COMB = (ps(n) for n in ("XT", "Z", "F", "PT", "OUT", "COMB"))
        W = ctx.enter_context(nc.psum_tensor("W", [P, 2, 512], fp32))

        consts = sem("consts")
        idx_in = sem("idx_in")
        zeroed_tile = sem("zeroed_tile")
        acc_zeroed = sem("acc_zeroed")
        prep = sem("prep")
        weights_scaled = sem("weights_scaled")
        gathered = [sem(f"gathered{s}") for s in range(UNROLL)]
        src_in = [sem(f"src_in{s}") for s in range(UNROLL)]
        e8_in = [sem(f"e8_in{s}") for s in range(UNROLL)]
        dstrow_in = [sem(f"dstrow_in{s}") for s in range(UNROLL)]
        scattered = [sem(f"scattered{j}") for j in range(2)]
        xt_ready, z_ready, f_ready, w_ready = sem("xt_ready"), sem("z_ready"), sem("f_ready"), sem("w_ready")
        prodt_ready, out_ready, comb_ready = sem("prodt_ready"), sem("out_ready"), sem("comb_ready")
        h_done, xt_copied, f_copied, pt_copied = sem("h_done"), sem("xt_copied"), sem("f_copied"), sem("pt_copied")
        out_copied, comb_copied = sem("out_copied"), sem("comb_copied")
        q_done, prod_done, feat_done = sem("q_done"), sem("prod_done"), sem("feat_done")
        same_done, row_done = sem("same_done"), sem("row_done")
        tm_done, ts_done, vq_done, cnt_done, shift_done = (sem(n) for n in ("tm_done", "ts_done", "vq_done", "cnt_done", "shift_done"))
        xn_in = [sem(f"xn_in{s}") for s in range(2)]
        acc_in = [sem(f"acc_in{s}") for s in range(2)]
        stored = [sem(f"stored{s}") for s in range(2)]
        xnt_ready, xnt_copied, sc_ready = sem("xnt_ready"), sem("xnt_copied"), sem("sc_ready")
        cs_done, red_done, abs_done, trig_done = sem("cs_done"), sem("red_done"), sem("abs_done"), sem("trig_done")
        mv_done, eps_done, rstd_done, norm_done = (sem(n) for n in ("mv_done", "eps_done", "rstd_done", "norm_done"))
        pool_passed, dve_passed, sp_passed = sem("pool_passed"), sem("dve_passed"), sem("sp_passed")
        ang_chain = sem("ang_chain")
        y_chain = sem("y_chain")
        stat_chain = sem("stat_chain")
        triga_done = sem("triga_done")
        block = ctx.enter_context(nc.Block())

        N_CONSTS = 10

        @block.sync
        def _(sp):
            for to, frm in ((ident_sb, ident), (later_sb, later), (fc_w1_sb, fc_w1), (fc_w2_sb, fc_w2),
                            (lin1_s_sb, lin1_s), (lin1_v_sb, lin1_v), (lin2_a_sb, lin2_a),
                            (lin2_b_sb, lin2_b), (sc_s_sb, sc_s), (sc_v_sb, sc_v)):
                sp.dma_start(to[:, :], frm).then_inc(consts, 16)

            sp.wait_ge(zeroed_tile, 1)
            reps = acc0.shape[0] // (3 * P)
            for a in accs:
                sp.dma_start(a.rearrange("(p r k) c -> p r (k c)", p=P, k=3),
                             zeros[:, :].rearrange("p (r c) -> p r c", r=1).to_broadcast([P, reps, 3 * ROWA])
                             ).then_inc(acc_zeroed, 16)

            def load(k):
                wait(sp, gathered[k.slot(UNROLL)], k.round(UNROLL) * 32)
                sp.sem_inc(sp_passed, 1)
                sp.dma_start(src_sb[:, k.slot(UNROLL), :], src[k.n, :, :]).then_inc(src_in[k.slot(UNROLL)], 16)
                wait(sp, z_ready, (k + (1 - UNROLL)).n)
                sp.sem_inc(sp_passed, 1)
                sp.dma_start(e8_sb[:, k.slot(UNROLL), :], ea8t[k.n, :, :]).then_inc(e8_in[k.slot(UNROLL)], 16)
                wait(sp, same_done, (k + (1 - UNROLL)).n)
                sp.sem_inc(sp_passed, 1)
                sp.dma_start(dstrow_sb[:, k.slot(UNROLL), :, :],
                             dst_rows[k.n, :, :].rearrange("(o j) e -> o j e", o=1).to_broadcast([P, 2, P])
                             ).then_inc(dstrow_in[k.slot(UNROLL)], 16)

            software_pipeline(sp, 0, NPAIR - 1, UNROLL, NPAIR - 1, load)

            def load_nodes(g, first=False):
                wait(sp, y_chain, (g + -1).n * (2 * G))
                sp.sem_inc(sp_passed, 1)
                sp.dma_start(xn_sb[:, g.slot(), :, :], xa_g[g.n, :, :]).then_inc(xn_in[g.slot()], 16)
                if first:
                    sp.wait_ge(scattered[0], 16 * NPAIR)
                    sp.wait_ge(scattered[1], 16 * NPAIR)
                wait(sp, cs_done, (g + -1).n)
                sp.sem_inc(sp_passed, 1)
                sp.dma_start(c0_sb[:, g.slot(), :, :], acc_g[0][g.n, :, :]).then_inc(acc_in[g.slot()], 16)
                sp.dma_start(c1_sb[:, g.slot(), :, :], acc_g[1][g.n, :, :]).then_inc(acc_in[g.slot()], 16)

            load_nodes(Step(None, 0), first=True)
            software_pipeline(sp, 1, NG - 1, 2, NG - 1, load_nodes)

        @block.gpsimd
        def _(pool):
            pool.memset(zeros[:, :], 0.0).then_inc(zeroed_tile, 1)
            pool.memset(half_pi[:, :], math.pi / 2).then_inc(prep, 1)
            pool.memset(minus_half[:, :], -0.5).then_inc(prep, 1)
            pool.iota(spare_row[:, :], pattern=[[0, NT]], base=NODES, channel_multiplier=1).then_inc(prep, 1)

            def step(k):
                g = k + 3
                if g.within(NPAIR):
                    wait(pool, xt_ready, (g + (1 - UNROLL)).n)
                    wait(pool, q_done, (g + (1 - UNROLL)).n)
                    wait(pool, src_in[g.slot(UNROLL)], (g.round(UNROLL) + 1) * 16)
                    pool.sem_inc(pool_passed, 1)
                    for j in range(2):
                        pool.indirect_dma_start(
                            out=x_sb[:, g.slot(UNROLL), j, :], out_offset=None, in_=xa,
                            in_offset=bass.IndirectOffsetOnAxis(ap=src_sb[:, g.slot(UNROLL), j:j + 1], axis=0),
                        ).then_inc(gathered[g.slot(UNROLL)], 16)
                s = k + -3
                if s.within(NPAIR):
                    if s.i is None and s.c == 0:
                        pool.wait_ge(acc_zeroed, 32)
                    pool.wait_ge(comb_copied, (s + 1).n)
                    pool.wait_ge(row_done, (s + 1).n)
                    for j in range(2):
                        wait(pool, scattered[j], s.n * 16)
                        pool.sem_inc(pool_passed, 1)
                        pool.indirect_dma_start(
                            out=accs[j], out_offset=bass.IndirectOffsetOnAxis(ap=row_sb[:, s.slot(UNROLL), j:j + 1], axis=0),
                            in_=comb_sb[:, s.slot(UNROLL), j, :], in_offset=None, compute_op=ALU.add,
                        ).then_inc(scattered[j], 16)

            software_pipeline(pool, -3, NPAIR + 2, 3, NPAIR - 4, step)

            def node_step(k):
                a = k + 1
                if a.within(NG):
                    wait(pool, acc_in[a.slot()], (a.round() + 1) * 32)
                    wait(pool, y_chain, (a + -1).n * (2 * G))
                    pool.tensor_tensor(out=cs_sb[:, a.slot(), :, :], in0=c0_sb[:, a.slot(), :, :],
                                       in1=c1_sb[:, a.slot(), :, :], op=ALU.add).then_inc(cs_done, 1)
                if k.within(NG):
                    pool.wait_ge(mv_done, (k + 1).n)
                    wait(pool, rstd_done, k.n)
                    pool.sem_inc(pool_passed, 1)
                    pool.tensor_scalar(vareps[:, :], meanvar[:, k.slot(), :, 1], EPS, None, ALU.add).then_inc(eps_done, 1)
                    pool.wait_ge(eps_done, (k + 1).n)
                    wait(pool, norm_done, (k + -1).n)
                    pool.tensor_tensor(out=rstd[:, k.slot(), :], in0=vareps[:, :], in1=minus_half[:, :],
                                       op=ALU.pow).then_inc(rstd_done, 1)

            software_pipeline(pool, -1, NG - 1, 1, NG - 2, node_step)

        @block.tensor
        def _(pe):
            pe.wait_ge(consts, 16 * N_CONSTS)
            pe.wait_ge(weights_scaled, 1)

            def step(k):
                e = k + -3
                if e.within(NPAIR):
                    pe.wait_ge(feat_done, (e + 1).n)
                    pe.wait_ge(same_done, (e + 1).n)
                    wait(pe, comb_copied, e.n)
                    for j in range(2):
                        last = nc.tensor.matmul(COMB[:, j * ROWA:(j + 1) * ROWA], same_sb[:, e.slot(), j, :],
                                                feat_sb[:, e.slot(), j, 0:ROWA], start=True, stop=True)
                    last.then_inc(comb_ready, 1)
                d = k + -2
                if d.within(NPAIR):
                    pe.wait_ge(pt_copied, (d + 1).n)
                    wait(pe, out_copied, d.n)
                    for j in range(2):
                        o = j * OUTW
                        nc.tensor.matmul(OUT[:, o:o + OUTW], pt_sb[:, d.slot(), (2 + j) * P:(3 + j) * P],
                                         lin2_b_sb[:, :], start=True, stop=False)
                        last = nc.tensor.matmul(OUT[:, o + NV:o + OUTW], pt_sb[:, d.slot(), j * P:(j + 1) * P],
                                                lin2_a_sb[:, :], start=False, stop=True)
                    last.then_inc(out_ready, 1)
                c = k + -1
                if c.within(NPAIR):
                    pe.wait_ge(prod_done, (c + 1).n)
                    wait(pe, pt_copied, c.n)
                    for j in range(2):
                        nc.tensor.transpose(PT[:, j * P:(j + 1) * P], pa_sb[:, c.slot(), j, :], ident_sb[:, :])
                    for j in range(2):
                        last = nc.tensor.transpose(PT[:, (2 + j) * P:(3 + j) * P], pb_sb[:, c.slot(), j, :], ident_sb[:, :])
                    last.then_inc(prodt_ready, 1)
                if k.within(NPAIR):
                    pe.wait_ge(xt_copied, (k + 1).n)
                    wait(pe, f_copied, k.n)
                    for j in range(2):
                        nc.tensor.matmul(F[:, j * ROW:j * ROW + NS], xt_sb[NS:P, k.slot(), (2 + j) * P:(3 + j) * P],
                                         lin1_s_sb[NS:P, :], start=True, stop=True)
                        last = nc.tensor.matmul(F[:, j * ROW + NS:(j + 1) * ROW],
                                                xt_sb[0:NV, k.slot(), j * P:(j + 1) * P],
                                                lin1_v_sb[:, :], start=True, stop=True)
                    last.then_inc(f_ready, 1)
                    pe.wait_ge(h_done, (k + 1).n)
                    wait(pe, prod_done, k.n)
                    for j in range(2):
                        last = nc.tensor.matmul(W[:, j, 0:NW], h_sb[j * NS:(j + 1) * NS, k.slot(), :],
                                                fc_w2_sb[j * NS:(j + 1) * NS, :], start=True, stop=True)
                    last.then_inc(w_ready, 1)
                a = k + 1
                if a.within(NPAIR):
                    wait(pe, e8_in[a.slot(UNROLL)], (a.round(UNROLL) + 1) * 16)
                    wait(pe, h_done, a.n)
                    for j in range(2):
                        last = nc.tensor.matmul(Z[j * NS:(j + 1) * NS, 0:P], fc_w1_sb[:, :],
                                                e8_sb[:, a.slot(UNROLL), j * P:(j + 1) * P], start=True, stop=True)
                    last.then_inc(z_ready, 1)
                    wait(pe, gathered[a.slot(UNROLL)], (a.round(UNROLL) + 1) * 32)
                    wait(pe, xt_copied, a.n)
                    for j in range(2):
                        nc.tensor.transpose(XT[:, j * P:(j + 1) * P], x_sb[:, a.slot(UNROLL), j, 0:P], ident_sb[:, :])
                        last = nc.tensor.transpose(XT[:, (2 + j) * P:(3 + j) * P], x_sb[:, a.slot(UNROLL), j, ROW - P:ROW], ident_sb[:, :])
                    last.then_inc(xt_ready, 1)

            software_pipeline(pe, -1, NPAIR + 2, 3, NPAIR - 2, step)

            pe.wait_ge(xt_copied, NPAIR)
            pe.wait_ge(pt_copied, NPAIR)
            pe.wait_ge(prod_done, NPAIR)

            def node_step(k):
                if k.within(NG):
                    pe.wait_ge(xnt_copied, (k + 1).n)
                    wait(pe, y_chain, k.n * (2 * G))
                    for j in range(G):
                        bank = W[:, j // 2, :]
                        o = j % 2 * ROW
                        nc.tensor.matmul(bank[:, o:o + NV], xnt_sb[0:NV, k.slot(), j // 2, (j % 2) * P:(1 + j % 2) * P],
                                         sc_v_sb[:, :], start=True, stop=True)
                        last = nc.tensor.matmul(bank[:, o + NV:o + ROW], xnt_sb[NS:P, k.slot(), j // 2, (2 + j % 2) * P:(3 + j % 2) * P],
                                                sc_s_sb[NS:P, :], start=True, stop=True)
                    last.then_inc(sc_ready, 1)
                a = k + 1
                if a.within(NG):
                    wait(pe, xn_in[a.slot()], (a.round() + 1) * 16)
                    wait(pe, xnt_copied, a.n)
                    for b in range(2):
                        bank = (XT, PT)[b]
                        for j in range(2):
                            nc.tensor.transpose(bank[:, j * P:(j + 1) * P], xn_sb[:, a.slot(), 2 * b + j, 0:P], ident_sb[:, :])
                            last = nc.tensor.transpose(bank[:, (2 + j) * P:(3 + j) * P],
                                                       xn_sb[:, a.slot(), 2 * b + j, ROW - P:ROW], ident_sb[:, :])
                    last.then_inc(xnt_ready, 1)

            software_pipeline(pe, -1, NG - 1, 1, NG - 2, node_step)

        @block.scalar
        def _(act):
            act.dma_start(dst_i[:, :], dst).then_inc(idx_in, 16)
            act.dma_start(ea4_sb[:, :, :], ea4).then_inc(idx_in, 16)

            def step(k):
                e = k + -3
                if e.within(NPAIR):
                    act.wait_ge(comb_ready, (e + 1).n)
                    for j in range(2):
                        wait(act, scattered[j], (e + (1 - UNROLL)).n * 16)
                    nc.scalar.copy(comb_sb[:, e.slot(UNROLL), :, :], COMB[:, 0:2 * ROWA].rearrange("p (j c) -> p j c", j=2)
                                   ).then_inc(comb_copied, 1)
                d = k + -2
                if d.within(NPAIR):
                    act.wait_ge(out_ready, (d + 1).n)
                    wait(act, comb_ready, (d + -1).n)
                    nc.scalar.copy(feat_sb[:, d.slot(), :, :], OUT[:, 0:2 * OUTW].rearrange("p (j c) -> p j c", j=2)
                                   ).then_inc(out_copied, 1)
                c = k + -1
                if c.within(NPAIR):
                    act.wait_ge(prodt_ready, (c + 1).n)
                    wait(act, out_ready, (c + -1).n)
                    nc.scalar.copy(pt_sb[:, c.slot(), :], PT[:, :]).then_inc(pt_copied, 1)
                if k.within(NPAIR):
                    act.wait_ge(f_ready, (k + 1).n)
                    wait(act, prod_done, (k + -1).n)
                    nc.scalar.copy(f_sb[:, k.slot(), :, :], F[:, 0:2 * ROW].rearrange("p (j c) -> p j c", j=2)
                                   ).then_inc(f_copied, 1)
                a = k + 1
                if a.within(NPAIR):
                    act.wait_ge(z_ready, (a + 1).n)
                    wait(act, w_ready, (a + -1).n)
                    nc.scalar.activation(h_sb[:, a.slot(), :], Z[:, 0:P], ACT.Silu, scale=1.0 / math.sqrt(8.0)
                                         ).then_inc(h_done, 1)
                    act.wait_ge(xt_ready, (a + 1).n)
                    nc.scalar.copy(xt_sb[:, a.slot(), :], XT[:, :]).then_inc(xt_copied, 1)

            software_pipeline(act, -1, NPAIR + 2, 6, NPAIR - 2, step)
            act.wait_ge(prep, 3)

            def node_step(k):
                a = k + 1
                if a.within(NG):
                    act.wait_ge(xnt_ready, (a + 1).n)
                    wait(act, sc_ready, (a + -1).n)
                    for b in range(2):
                        last = nc.scalar.copy(xnt_sb[:, a.slot(), b, :], (XT, PT)[b][:, :])
                    last.then_inc(xnt_copied, 1)
                s = k + -1
                if s.within(NG):
                    act.wait_ge(norm_done, (s + 1).n)
                    act.dma_start(out_g[s.n, :, :], y_sb[:, s.slot(), :, :]).then_inc(stored[s.slot()], 16)
                if a.within(NG):
                    act.wait_ge(red_done, (a + 1).n)
                    wait(act, triga_done, (a + -1).n)
                    nc.scalar.activation(redabs[:, :], red[:, a.slot(), :], ACT.Abs).then_inc(abs_done, 1)
                    nc.scalar.activation(trig[:, a.slot(), 1, :], red[:, a.slot(), :], ACT.Sin)
                    act.wait_ge(abs_done, (a + 1).n)
                    nc.scalar.activation(trig[:, a.slot(), 0, :], redabs[:, :], ACT.Sin, bias=half_pi[:, :], scale=-1.0
                                         ).then_inc(trig_done, 1)

            software_pipeline(act, -1, NG, 1, NG - 2, node_step)
            for s in range(2):
                act.wait_ge(stored[s], 16 * ((NG + 1 - s) // 2))

        @block.vector
        def _(dve):
            dve.wait_ge(consts, 16 * N_CONSTS)
            s64, s32 = 1.0 / math.sqrt(NS), 1.0 / math.sqrt(MU)
            s96 = 1.0 / math.sqrt(NS + MU) / math.sqrt(NEIGHBORS)
            for w, s in ((fc_w2_sb, s64), (lin1_s_sb, s64), (lin1_v_sb, s32), (sc_s_sb, s64), (sc_v_sb, s32),
                         (lin2_a_sb, s96), (lin2_b_sb, s96)):
                last = nc.vector.tensor_scalar(w[:, :], w[:, :], s, None, ALU.mult)
            last.then_inc(ang_chain, 1)
            dve.wait_ge(ang_chain, 1)
            nc.vector.tensor_scalar(lin2_a_sb[0:NS, NS:NS + 1], lin2_a_sb[0:NS, NS:NS + 1], 0.1, None, ALU.mult)
            nc.vector.tensor_scalar(lin2_b_sb[NV:P, :], lin2_b_sb[NV:P, :], 1.0 / math.sqrt(3.0), None,
                                    ALU.mult).then_inc(ang_chain, 1)
            dve.wait_ge(ang_chain, 2)
            nc.vector.tensor_scalar(lin2_b_sb[NV:P, ROW:ROWA], lin2_b_sb[NV:P, ROW:ROWA], 0.1, None,
                                    ALU.mult).then_inc(weights_scaled, 1)
            dve.wait_ge(idx_in, 32)
            nc.vector.tensor_copy(dst_f[:, :], dst_i[:, :]).then_inc(ang_chain, 1)
            dve.wait_ge(ang_chain, 3)
            dve.wait_ge(prep, 3)
            nc.vector.tensor_tensor(to_spare[:, :], spare_row[:, :], dst_f[:, :], ALU.subtract).then_inc(ang_chain, 1)
            dve.wait_ge(ang_chain, 4)

            def step(k):
                d = k + -2
                if d.within(NPAIR):
                    o = feat_sb[:, d.slot(), :, :]
                    dve.wait_ge(out_copied, (d + 1).n)
                    nc.vector.tensor_tensor(
                        vq_sb[:, :, :, :],
                        o[:, :, ROWA:OUTW].rearrange("p j (c o) -> p j c o", o=1).to_broadcast([P, 2, MU, 3]),
                        q_sb[:, d.slot(), :, 1:4].rearrange("p j (o c) -> p j o c", o=1).to_broadcast([P, 2, MU, 3]),
                        ALU.mult).then_inc(vq_done, 1)
                    wait(dve, dstrow_in[d.slot(UNROLL)], (d.round(UNROLL) + 1) * 16)
                    wait(dve, comb_ready, (d + -1).n)
                    for j in range(2):
                        last = nc.vector.tensor_scalar(same_sb[:, d.slot(), j, :], dstrow_sb[:, d.slot(UNROLL), j, :],
                                                       dst_f[:, bass.ds(d.n * 2 + j, 1)], None, ALU.is_equal)
                    last.then_inc(same_done, 1)
                    dve.wait_ge(vq_done, (d + 1).n)
                    nc.vector.tensor_tensor(o[:, :, 0:NV], o[:, :, 0:NV],
                                            vq_sb[:, :, :, :].rearrange("p j c o -> p j (c o)"),
                                            ALU.add).then_inc(feat_done, 1)
                    dve.wait_ge(same_done, (d + 1).n)
                    for j in range(2):
                        last = nc.vector.tensor_tensor_reduce(
                            out=junk_sb[:, j, :], in0=same_sb[:, d.slot(), j, :], in1=later_sb[:, :], scale=1.0,
                            scalar=0.0, op0=ALU.mult, op1=ALU.add, accum_out=later_cnt[:, d.slot(), j:j + 1])
                    last.then_inc(cnt_done, 1)
                if d.within(NPAIR):
                    dve.wait_ge(cnt_done, (d + 1).n)
                    nc.vector.scalar_tensor_tensor(shift_sb[:, d.slot(), :], later_cnt[:, d.slot(), :], 1.0,
                                                   to_spare[:, bass.ds(d.n * 2, 2)], ALU.min, ALU.mult
                                                   ).then_inc(shift_done, 1)
                if k.within(NPAIR):
                    wait(dve, gathered[k.slot(UNROLL)], (k.round(UNROLL) + 1) * 32)
                    nc.vector.tensor_tensor(q_sb[:, k.slot(), :, :], ea4_sb[:, bass.ds(k.n * 2, 2), :],
                                            x_sb[:, k.slot(UNROLL), :, ROW:ROWA].to_broadcast([P, 2, 4]),
                                            ALU.mult).then_inc(q_done, 1)
                if d.within(NPAIR):
                    dve.wait_ge(shift_done, (d + 1).n)
                    for j in range(2):
                        wait(dve, scattered[j], (d + (1 - UNROLL)).n * 16)
                    nc.vector.tensor_tensor(row_sb[:, d.slot(UNROLL), :], shift_sb[:, d.slot(), :],
                                            dst_f[:, bass.ds(d.n * 2, 2)], ALU.add).then_inc(row_done, 1)
                if k.within(NPAIR):
                    f, q = f_sb[:, k.slot(), :, :], q_sb[:, k.slot(), :, :]
                    w = W[:, :, 0:NW]
                    dve.wait_ge(q_done, (k + 1).n)
                    dve.wait_ge(f_copied, (k + 1).n)
                    nc.vector.tensor_tensor(tm_sb[:, :, :, :], f[:, :, NS:ROW].rearrange("p j (d c) -> p j d c", d=3),
                                            q[:, :, 1:4].rearrange("p j (d o) -> p j d o", o=1).to_broadcast([P, 2, 3, MU]),
                                            ALU.mult).then_inc(tm_done, 1)
                    dve.wait_ge(w_ready, (k + 1).n)
                    wait(dve, prodt_ready, (k + -1).n)
                    for j in range(2):
                        nc.vector.scalar_tensor_tensor(pa_sb[:, k.slot(), j, 0:NS], f[:, j, 0:NS], q[:, j, 0:1],
                                                       w[:, j, 0:NS], ALU.mult, ALU.mult)
                    dve.wait_ge(tm_done, (k + 1).n)
                    nc.vector.tensor_reduce(ts_sb[:, :, :], tm_sb[:, :, :, :].rearrange("p j d c -> p j c d"),
                                            mybir.AxisListType.X, ALU.add).then_inc(ts_done, 1)
                    for j in range(2):
                        nc.vector.scalar_tensor_tensor(
                            pb_sb[:, k.slot(), j, 0:NV].rearrange("p (d c) -> p d c", d=3),
                            f[:, j, NS:ROW].rearrange("p (d c) -> p d c", d=3), q[:, j, 0:1],
                            w[:, j, 2 * NS:2 * NS + MU].rearrange("p (o c) -> p o c", o=1).to_broadcast([P, 3, MU]),
                            ALU.mult, ALU.mult)
                    nc.vector.tensor_tensor(pa_sb[:, k.slot(), :, NS:P], f[:, :, 0:NS], w[:, :, NS:2 * NS], ALU.mult)
                    dve.wait_ge(ts_done, (k + 1).n)
                    nc.vector.tensor_tensor(pb_sb[:, k.slot(), :, NV:P], ts_sb[:, :, :], w[:, :, 2 * NS + MU:NW],
                                            ALU.mult).then_inc(prod_done, 1)

            software_pipeline(dve, 0, NPAIR + 1, 5, NPAIR - 1, step)

            C1, C2, C3 = 6.28125, 0.0019350051879882812, 3.019916050561733e-07
            MAGIC = 1.5 * 2.0 ** 23
            PI = 3.1415925
            LINKS = 6

            def node_step(k):
                if k.within(NG):
                    dve.wait_ge(trig_done, (k + 1).n)
                    attr = xn_sb[:, k.slot(), :, ROW:ROWA].rearrange("p g o -> p o g")
                    nc.vector.tensor_tensor(trig_a[:, :, :], trig[:, k.slot(), :, :], attr.to_broadcast([P, 2, G]),
                                            ALU.mult).then_inc(triga_done, 1)
                    dve.wait_ge(triga_done, (k + 1).n)
                    dve.wait_ge(sc_ready, (k + 1).n)
                    wait(dve, stored[k.slot()], k.round() * 16)
                    for j in range(G):
                        o = j % 2 * ROW
                        nc.vector.scalar_tensor_tensor(y_sb[:, k.slot(), j, :], W[:, j // 2, o:o + ROW],
                                                       trig_a[:, 0, j:j + 1], xn_sb[:, k.slot(), j, 0:ROW],
                                                       ALU.mult, ALU.add).then_inc(y_chain, 1)
                    for j in range(G):
                        dve.wait_ge(y_chain, k.n * 2 * G + (j + 1))
                        last = nc.vector.scalar_tensor_tensor(y_sb[:, k.slot(), j, :], cs_sb[:, k.slot(), j, 0:ROW],
                                                              trig_a[:, 1, j:j + 1], y_sb[:, k.slot(), j, :],
                                                              ALU.mult, ALU.add).then_inc(y_chain, 1)
                    for j in range(G):
                        dve.wait_ge(y_chain, k.n * 2 * G + G + (j + 1))
                        last = nc.vector.bn_stats(stats[:, j, :], y_sb[:, k.slot(), j, :])
                        last.then_inc(stat_chain, 1)
                    for j in range(G):
                        dve.wait_ge(stat_chain, k.n * G + (j + 1))
                        dve.sem_inc(dve_passed, 1)
                        last = nc.vector.bn_aggr(meanvar[:, k.slot(), j, :], stats[:, j, :])
                    last.then_inc(mv_done, 1)
                a = k + 1
                if a.within(NG):
                    dve.wait_ge(cs_done, (a + 1).n)
                    wait(dve, xn_in[a.slot()], (a.round() + 1) * 16)
                    at = a.n * LINKS
                    nc.vector.tensor_tensor(ang[:, :], cs_sb[:, a.slot(), :, ROW], xn_sb[:, a.slot(), :, ROW],
                                            ALU.mult).then_inc(ang_chain, 1)
                    dve.wait_ge(ang_chain, at + 5)
                    nc.vector.tensor_scalar(turns[:, :], ang[:, :], 1.0 / (2.0 * math.pi), MAGIC, ALU.mult, ALU.add
                                            ).then_inc(ang_chain, 1)
                    dve.wait_ge(ang_chain, at + 6)
                    nc.vector.tensor_scalar(turns[:, :], turns[:, :], MAGIC, None, ALU.subtract).then_inc(ang_chain, 1)
                    for n, c in enumerate((C1, C2, C3)):
                        dve.wait_ge(ang_chain, at + 7 + n)
                        nc.vector.scalar_tensor_tensor(ang[:, :], turns[:, :], -c, ang[:, :], ALU.mult, ALU.add
                                                       ).then_inc(ang_chain, 1)
                    dve.wait_ge(ang_chain, at + 10)
                    wait(dve, trig_done, (a + -1).n)
                    nc.vector.tensor_scalar(red[:, a.slot(), :], ang[:, :], -PI, PI, ALU.max, ALU.min
                                            ).then_inc(red_done, 1)
                b = k + -1
                if b.within(NG):
                    dve.wait_ge(rstd_done, (b + 1).n)
                    for j in range(G):
                        last = nc.vector.tensor_scalar(y_sb[:, b.slot(), j, :], y_sb[:, b.slot(), j, :],
                                                       meanvar[:, b.slot(), j, 0:1], rstd[:, b.slot(), j:j + 1],
                                                       ALU.subtract, ALU.mult)
                    last.then_inc(norm_done, 1)

            software_pipeline(dve, -1, NG, 1, NG - 2, node_step)


def layouts(x, src, dst, edge_attr_4, edge_attr_8, node_vec1, sc_w0, sc_w1, lin1_w0, lin1_w1, fc_w1,
            fc_w2, lin2_w0, lin2_w1, lin3_w, tiles):
    n, e = x.shape[0], src.shape[0]
    rows = tiles * P
    f32 = np.float32
    xa = np.zeros((rows, ROWA), f32)
    xa[:n, :NV], xa[:n, NV:ROW], xa[:n, ROW] = x[:, NS:], x[:, :NS], node_vec1[:, 0]
    src_p = np.zeros(rows, np.int32)
    src_p[:e] = src
    dst_p = np.full(rows, n, np.int32)
    dst_p[:e] = dst
    ea4 = np.zeros((rows, 4), f32)
    ea4[:e] = edge_attr_4
    ea8 = np.zeros((rows, 8), f32)
    ea8[:e] = edge_attr_8

    def by_component(w, rows_grouped, cols_grouped):
        u, c = w.shape
        m = np.zeros((u, 3, c, 3), f32)
        for d in range(3):
            m[:, d, :, d] = w
        if rows_grouped:
            m = m.transpose(1, 0, 2, 3).reshape(3 * u, c, 3)
        else:
            m = m.reshape(3 * u, c, 3)
        if cols_grouped:
            m = m.transpose(0, 2, 1)
        return np.ascontiguousarray(m.reshape(3 * u, 3 * c))

    lin2_a = np.zeros((P, NS + 1 + MU), f32)
    lin2_a[:NS, :NS] = lin2_w0[:NS]
    lin2_a[:NS, NS] = lin3_w[:NS, 0]
    lin2_a[NS:, NS + 1:] = lin2_w1[:NS]
    lin2_b = np.zeros((P, OUTW), f32)
    lin2_b[:NV, :NV] = by_component(lin2_w1[NS:], True, False)
    lin2_b[NV:, NV:ROW] = lin2_w0[NS:]
    lin2_b[NV:, ROW] = lin3_w[NS:, 0]
    order = np.arange(P)
    return {
        "xa": xa,
        "src": np.ascontiguousarray(src_p.reshape(P, tiles // 2, 2).transpose(1, 0, 2)),
        "dst": dst_p.reshape(P, tiles),
        "dst_rows": np.ascontiguousarray(dst_p.reshape(P, tiles).T).reshape(tiles // 2, 2, P),
        "ea4": ea4.reshape(P, tiles, 4),
        "ea8t": np.ascontiguousarray(ea8.reshape(P, tiles // 2, 2, 8).transpose(1, 3, 2, 0)).reshape(tiles // 2, 8, 2 * P),
        "fc_w1": np.asarray(fc_w1),
        "fc_w2": np.concatenate([fc_w2, fc_w2]),
        "lin1_s": np.concatenate([lin1_w0, lin1_w0]),
        "lin1_v": by_component(lin1_w1, False, True),
        "lin2_a": lin2_a,
        "lin2_b": lin2_b,
        "sc_s": np.concatenate([sc_w0, sc_w0]),
        "sc_v": by_component(sc_w1, False, False),
        "ident": np.eye(P, dtype=f32),
        "later": (order[None, :] > order[:, None]).astype(f32),
    }


def kernel(x, src, dst, edge_attr_4, edge_attr_8, node_vec1, L0_gnn_sc_w0, L0_gnn_sc_w1, L0_gnn_lin1_w0,
           L0_gnn_lin1_w1, L0_gnn_fc_w1, L0_gnn_fc_w2, L0_gnn_lin2_w0, L0_gnn_lin2_w1, L0_gnn_lin3_w):
    import concourse.bacc as bacc
    from concourse.bass_utils import run_bass_kernel_spmd

    n = x.shape[0]
    tiles = -(-max(n + 1, src.shape[0]) // (P * 2 * G)) * 2 * G
    arrays = layouts(*(np.asarray(a) for a in (
        x, src, dst, edge_attr_4, edge_attr_8, node_vec1, L0_gnn_sc_w0, L0_gnn_sc_w1, L0_gnn_lin1_w0,
        L0_gnn_lin1_w1, L0_gnn_fc_w1, L0_gnn_fc_w2, L0_gnn_lin2_w0, L0_gnn_lin2_w1, L0_gnn_lin3_w)), tiles)
    nc = bacc.Bacc("TRN2", target_bir_lowering=False, num_devices=1)
    args = {k: nc.dram_tensor(k, a.shape, mybir.dt.from_np(a.dtype), kind="ExternalInput").ap()
            for k, a in arrays.items()}
    for k in ("acc0", "acc1"):
        args[k] = nc.dram_tensor(k, [(tiles + 1) * P, ROWA], mybir.dt.float32, kind="Internal").ap()
    args["out"] = nc.dram_tensor("out", [tiles * P, ROW], mybir.dt.float32, kind="ExternalOutput").ap()
    gnn_program(nc, **args)
    r = run_bass_kernel_spmd(nc, [arrays], core_ids=[0])
    got = r.results[0]["out"][:n]
    return np.concatenate([got[:, NV:], got[:, :NV]], axis=1)
```

```python
import concourse.bass as bass
from concourse import mybir
from contextlib import ExitStack
import math
import numpy as np

P = 128
NS, NV, MU = 64, 96, 32
ROW = NS + NV
ROWA = ROW + 1
NW = 2 * NS + 2 * MU
OUTW = ROWA + MU
G = 4
SPARE = 8
EPS = 1e-5
NEIGHBORS = 16.0


UNROLL = 4


class Step:

    def __init__(self, i, c):
        self.i, self.c = i, c
        self.n = c if i is None else i * UNROLL + c

    def __add__(self, d):
        return Step(self.i, self.c + d)

    def slot(self, slots=2):
        return self.c % slots

    def round(self, slots=2):
        return self.c // slots if self.i is None else self.i * (UNROLL // slots) + self.c // slots

    def within(self, count):
        return self.i is not None or 0 <= self.c < count


def wait(eng, sem, count):
    if not isinstance(count, int) or count > 0:
        eng.wait_ge(sem, count)


def software_pipeline(eng, first, last, fill, drain, step):
    count = max(drain - fill + 1, 0) // UNROLL
    for k in range(first, fill):
        step(Step(None, k))
    if count:
        with eng.Fori(0, count, 1) as i:
            for u in range(UNROLL):
                step(Step(i, fill + u))
    for k in range(fill + UNROLL * count, last + 1):
        step(Step(None, k))


def gnn_program(nc, xa, x_last, src, dst, dst_rows, ea4, ea8t, fc_w1, fc_w2, lin1_s, lin1_v, lin2_a, lin2_b,
                sc_a, sc_b, ident, later, acc, out):
    fp32, i32 = mybir.dt.float32, mybir.dt.int32
    ALU, ACT = mybir.AluOpType, mybir.ActivationFunctionType
    NT = dst.shape[1]
    NPAIR = NT // 2
    NG = NT // G
    NODES = NT * P
    xa_g = xa.rearrange("(g p j) c -> g p (j c)", p=P, j=G)
    out_g = out.rearrange("(g p j) c -> g p (j c)", p=P, j=G)
    acc_g = acc[0:NODES, :].rearrange("(g p j) c -> g p (j c)", p=P, j=G)

    with ExitStack() as ctx:
        def sb(name, shape, dt=fp32):
            return ctx.enter_context(nc.sbuf_tensor(name, shape, dt))

        def ps(name):
            return ctx.enter_context(nc.psum_tensor(name, [P, 512], fp32))

        def sem(name):
            return ctx.enter_context(nc.semaphore(name))

        ident_sb = sb("ident_sb", [P, P])
        later_sb = sb("later_sb", [P, 2 * P])
        fc_w1_sb = sb("fc_w1_sb", [8, NS])
        fc_w2_sb = sb("fc_w2_sb", [P, NW])
        lin1_s_sb = sb("lin1_s_sb", [P, NS])
        lin1_v_sb = sb("lin1_v_sb", [NV, NV])
        lin2_a_sb = sb("lin2_a_sb", [P, NS + 1 + MU])
        lin2_b_sb = sb("lin2_b_sb", [P, OUTW])
        sc_a_sb = sb("sc_a_sb", [P, ROW])
        sc_b_sb = sb("sc_b_sb", [P, NS])
        half_pi = sb("half_pi", [P, 1])
        minus_half = sb("minus_half", [P, G])
        dst_i = sb("dst_i", [P, NT], i32)
        dst_f = sb("dst_f", [P, NT])
        spare_row = sb("spare_row", [P, NT], i32)
        to_spare = sb("to_spare", [P, NT])
        ea4_sb = sb("ea4_sb", [P, NT, 4])
        zeros = sb("zeros", [P, SPARE * ROWA])
        src_sb = sb("src_sb", [P, UNROLL, 2], i32)
        x_sb = sb("x_sb", [P, UNROLL, 2, ROWA])
        e8_sb = sb("e8_sb", [8, UNROLL, 2 * P])
        dstrow_sb = sb("dstrow_sb", [P, UNROLL, 2, P], i32)
        xt_sb = sb("xt_sb", [P, 2, 4 * P])
        h_sb = sb("h_sb", [P, 2, P])
        f_sb = sb("f_sb", [P, 2, 2, ROW])
        q_sb = sb("q_sb", [P, UNROLL, 2, 4])
        tm_sb = sb("tm_sb", [P, 2, 3, MU])
        ts_sb = sb("ts_sb", [P, 2, MU])
        pa_sb = sb("pa_sb", [P, 2, 2, P])
        pb_sb = sb("pb_sb", [P, 2, 2, P])
        pt_sb = sb("pt_sb", [P, 2, 4 * P])
        vq_sb = sb("vq_sb", [P, 2, MU, 3])
        feat_sb = sb("feat_sb", [P, UNROLL, 2, OUTW])
        same_sb = sb("same_sb", [P, 2, 3, P])
        junk_sb = sb("junk_sb", [P, 3, P])
        later_cnt = sb("later_cnt", [P, 2, 2])
        shift_sb = sb("shift_sb", [P, 2, 2])
        row_sb = sb("row_sb", [P, UNROLL, 2], i32)
        comb_sb = sb("comb_sb", [P, UNROLL, 2, ROWA])
        xn_sb = sb("xn_sb", [P, UNROLL, G, ROWA])
        cs_sb = sb("cs_sb", [P, UNROLL, G, ROWA])
        xl_sb = sb("xl_sb", [P, UNROLL, P])
        xnt_a_sb = sb("xnt_a_sb", [P, 2, G, P])
        xnt_b_sb = sb("xnt_b_sb", [P, 2, P])
        y_sb = sb("y_sb", [P, UNROLL, G, ROW])
        ang = sb("ang", [P, 2, G])
        turns = sb("turns", [P, 2, G])
        red = sb("red", [P, 2, G])
        redabs = sb("redabs", [P, 2, G])
        trig = sb("trig", [P, 2, 2, G])
        trig_a = sb("trig_a", [P, 2, 2, G])
        stats = sb("stats", [P, G, 6])
        meanvar = sb("meanvar", [P, UNROLL, G, 2])
        vareps = sb("vareps", [P, G])
        rstd = sb("rstd", [P, UNROLL, G])
        minus_mean = sb("minus_mean", [P, G])
        shift = sb("shift", [P, UNROLL, G])
        XT, Z, F, PT, OUT, COMB = (ps(n) for n in ("XT", "Z", "F", "PT", "OUT", "COMB"))
        W = ctx.enter_context(nc.psum_tensor("W", [P, 2, 512], fp32))

        xnt_banks = ((XT, PT), (F, Z))
        sc_banks = (W[:, 0, :], W[:, 1, :], OUT, COMB)

        consts = sem("consts")
        idx_in = sem("idx_in")
        zeroed_tile = sem("zeroed_tile")
        acc_zeroed = sem("acc_zeroed")
        prep = sem("prep")
        weights_scaled = sem("weights_scaled")
        gathered = [sem(f"gathered{s}") for s in range(UNROLL)]
        src_in = [sem(f"src_in{s}") for s in range(UNROLL)]
        e8_in = [sem(f"e8_in{s}") for s in range(UNROLL)]
        dstrow_in = [sem(f"dstrow_in{s}") for s in range(UNROLL)]
        scattered = [sem(f"scattered{j}") for j in range(2)]
        xt_ready, z_ready, f_ready, w_ready = sem("xt_ready"), sem("z_ready"), sem("f_ready"), sem("w_ready")
        prodt_ready, out_ready, comb_ready = sem("prodt_ready"), sem("out_ready"), sem("comb_ready")
        h_done, xt_copied, f_copied, pt_copied = sem("h_done"), sem("xt_copied"), sem("f_copied"), sem("pt_copied")
        out_copied, comb_copied = sem("out_copied"), sem("comb_copied")
        q_done, prod_done, feat_done = sem("q_done"), sem("prod_done"), sem("feat_done")
        same_done, row_done = sem("same_done"), sem("row_done")
        tm_done, ts_done, vq_done, cnt_done, spare_done = (sem(n) for n in ("tm_done", "ts_done", "vq_done", "cnt_done", "spare_done"))
        xn_in = [sem(f"xn_in{s}") for s in range(UNROLL)]
        xl_in = [sem(f"xl_in{s}") for s in range(UNROLL)]
        acc_in = [sem(f"acc_in{s}") for s in range(UNROLL)]
        stored = [sem(f"stored{s}") for s in range(UNROLL)]
        xnt_ready, xnt_copied, sc_ready = sem("xnt_ready"), sem("xnt_copied"), sem("sc_ready")
        red_done, abs_done, trig_done = sem("red_done"), sem("abs_done"), sem("trig_done")
        mv_done, eps_done, rstd_done, norm_done = (sem(n) for n in ("mv_done", "eps_done", "rstd_done", "norm_done"))
        pool_passed, dve_passed, sp_passed = sem("pool_passed"), sem("dve_passed"), sem("sp_passed")
        ang_chain = sem("ang_chain")
        y_chain = sem("y_chain")
        stat_chain = sem("stat_chain")
        triga_done = sem("triga_done")
        shift_done = sem("shift_done")
        block = ctx.enter_context(nc.Block())

        N_CONSTS = 10

        @block.sync
        def _(sp):
            for to, frm in ((ident_sb, ident), (later_sb, later), (fc_w1_sb, fc_w1), (fc_w2_sb, fc_w2),
                            (lin1_s_sb, lin1_s), (lin1_v_sb, lin1_v), (lin2_a_sb, lin2_a),
                            (lin2_b_sb, lin2_b), (sc_a_sb, sc_a), (sc_b_sb, sc_b)):
                sp.dma_start(to[:, :], frm).then_inc(consts, 16)

            sp.wait_ge(zeroed_tile, 1)
            reps = acc.shape[0] // (SPARE * P)
            sp.dma_start(acc.rearrange("(p r k) c -> p r (k c)", p=P, k=SPARE),
                         zeros[:, :].rearrange("p (r c) -> p r c", r=1).to_broadcast([P, reps, SPARE * ROWA])
                         ).then_inc(acc_zeroed, 16)

            def load(k):
                wait(sp, gathered[k.slot(UNROLL)], k.round(UNROLL) * 32)
                sp.sem_inc(sp_passed, 1)
                sp.dma_start(src_sb[:, k.slot(UNROLL), :], src[k.n, :, :]).then_inc(src_in[k.slot(UNROLL)], 16)
                wait(sp, z_ready, (k + (1 - UNROLL)).n)
                sp.sem_inc(sp_passed, 1)
                sp.dma_start(e8_sb[:, k.slot(UNROLL), :], ea8t[k.n, :, :]).then_inc(e8_in[k.slot(UNROLL)], 16)
                wait(sp, same_done, (k + (1 - UNROLL)).n)
                sp.sem_inc(sp_passed, 1)
                sp.dma_start(dstrow_sb[:, k.slot(UNROLL), :, :],
                             dst_rows[k.n, :, :].rearrange("(o j) e -> o j e", o=1).to_broadcast([P, 2, P])
                             ).then_inc(dstrow_in[k.slot(UNROLL)], 16)

            software_pipeline(sp, 0, NPAIR - 1, UNROLL, NPAIR - 1, load)

            def load_nodes(g, first=False):
                wait(sp, y_chain, (g + (1 - UNROLL)).n * (2 * G))
                sp.sem_inc(sp_passed, 1)
                sp.dma_start(xn_sb[:, g.slot(UNROLL), :, :], xa_g[g.n, :, :]).then_inc(xn_in[g.slot(UNROLL)], 16)
                sp.dma_start(xl_sb[:, g.slot(UNROLL), :], x_last[g.n, :, :]).then_inc(xl_in[g.slot(UNROLL)], 16)
                if first:
                    sp.wait_ge(scattered[0], 16 * NPAIR)
                    sp.wait_ge(scattered[1], 16 * NPAIR)
                sp.dma_start(cs_sb[:, g.slot(UNROLL), :, :], acc_g[g.n, :, :]).then_inc(acc_in[g.slot(UNROLL)], 16)

            load_nodes(Step(None, 0), first=True)
            software_pipeline(sp, 1, NG - 1, UNROLL, NG - 1, load_nodes)

        @block.gpsimd
        def _(pool):
            pool.memset(zeros[:, :], 0.0).then_inc(zeroed_tile, 1)
            pool.memset(half_pi[:, :], math.pi / 2).then_inc(prep, 1)
            pool.memset(minus_half[:, :], -0.5).then_inc(prep, 1)
            pool.iota(spare_row[:, :], pattern=[[0, NPAIR], [P, 2]], base=NODES, channel_multiplier=1).then_inc(prep, 1)

            def step(k):
                s = k + -4
                if s.within(NPAIR):
                    if s.i is None and s.c == 0:
                        pool.wait_ge(acc_zeroed, 16)
                    pool.wait_ge(comb_copied, (s + 1).n)
                    pool.wait_ge(row_done, (s + 1).n)
                    for j in range(2):
                        wait(pool, scattered[j], s.n * 16)
                    pool.sem_inc(pool_passed, 1)
                    for j in range(2):
                        pool.indirect_dma_start(
                            out=acc, out_offset=bass.IndirectOffsetOnAxis(ap=row_sb[:, s.slot(UNROLL), j:j + 1], axis=0),
                            in_=comb_sb[:, s.slot(UNROLL), j, :], in_offset=None, compute_op=ALU.add,
                        ).then_inc(scattered[j], 16)
                g = k + 3
                if g.within(NPAIR):
                    wait(pool, xt_ready, (g + (1 - UNROLL)).n)
                    wait(pool, q_done, (g + (1 - UNROLL)).n)
                    wait(pool, src_in[g.slot(UNROLL)], (g.round(UNROLL) + 1) * 16)
                    pool.sem_inc(pool_passed, 1)
                    for j in range(2):
                        pool.indirect_dma_start(
                            out=x_sb[:, g.slot(UNROLL), j, :], out_offset=None, in_=xa,
                            in_offset=bass.IndirectOffsetOnAxis(ap=src_sb[:, g.slot(UNROLL), j:j + 1], axis=0),
                        ).then_inc(gathered[g.slot(UNROLL)], 16)

            software_pipeline(pool, -3, NPAIR + 3, 4, NPAIR - 4, step)

            def node_step(k):
                pool.wait_ge(mv_done, (k + 1).n)
                wait(pool, shift_done, k.n)
                wait(pool, norm_done, (k + (1 - UNROLL)).n)
                pool.sem_inc(pool_passed, 1)
                s = k.slot(UNROLL)
                pool.tensor_scalar(vareps[:, :], meanvar[:, s, :, 1], EPS, None, ALU.add).then_inc(eps_done, 1)
                pool.tensor_scalar(minus_mean[:, :], meanvar[:, s, :, 0], -1.0, None, ALU.mult)
                pool.wait_ge(eps_done, (k + 1).n)
                pool.tensor_tensor(out=rstd[:, s, :], in0=vareps[:, :], in1=minus_half[:, :],
                                   op=ALU.pow).then_inc(rstd_done, 1)
                pool.wait_ge(rstd_done, (k + 1).n)
                pool.tensor_tensor(out=shift[:, s, :], in0=minus_mean[:, :], in1=rstd[:, s, :],
                                   op=ALU.mult).then_inc(shift_done, 1)

            software_pipeline(pool, 0, NG - 1, UNROLL, NG - 1, node_step)

        @block.tensor
        def _(pe):
            pe.wait_ge(consts, 16 * N_CONSTS)
            pe.wait_ge(weights_scaled, 1)

            def step(k):
                e = k + -4
                if e.within(NPAIR):
                    pe.wait_ge(feat_done, (e + 1).n)
                    pe.wait_ge(same_done, (e + 1).n)
                    wait(pe, comb_copied, e.n)
                    for j, b, f, start in ((0, 0, 0, True), (1, 1, 0, True), (1, 2, 1, False)):
                        last = nc.tensor.matmul(COMB[:, j * ROWA:(j + 1) * ROWA], same_sb[:, e.slot(), b, :],
                                                feat_sb[:, e.slot(UNROLL), f, 0:ROWA], start=start, stop=j == 0 or not start)
                    last.then_inc(comb_ready, 1)
                d = k + -2
                if d.within(NPAIR):
                    pe.wait_ge(pt_copied, (d + 1).n)
                    wait(pe, out_copied, d.n)
                    for j in range(2):
                        o = j * OUTW
                        nc.tensor.matmul(OUT[:, o:o + OUTW], pt_sb[:, d.slot(), (2 + j) * P:(3 + j) * P],
                                         lin2_b_sb[:, :], start=True, stop=False)
                        last = nc.tensor.matmul(OUT[:, o + NV:o + OUTW], pt_sb[:, d.slot(), j * P:(j + 1) * P],
                                                lin2_a_sb[:, :], start=False, stop=True)
                    last.then_inc(out_ready, 1)
                c = k + -1
                if c.within(NPAIR):
                    pe.wait_ge(prod_done, (c + 1).n)
                    wait(pe, pt_copied, c.n)
                    for j in range(2):
                        nc.tensor.transpose(PT[:, j * P:(j + 1) * P], pa_sb[:, c.slot(), j, :], ident_sb[:, :])
                    for j in range(2):
                        last = nc.tensor.transpose(PT[:, (2 + j) * P:(3 + j) * P], pb_sb[:, c.slot(), j, :], ident_sb[:, :])
                    last.then_inc(prodt_ready, 1)
                if k.within(NPAIR):
                    pe.wait_ge(xt_copied, (k + 1).n)
                    wait(pe, f_copied, k.n)
                    for j in range(2):
                        nc.tensor.matmul(F[:, j * ROW:j * ROW + NS], xt_sb[NS:P, k.slot(), (2 + j) * P:(3 + j) * P],
                                         lin1_s_sb[NS:P, :], start=True, stop=True)
                        last = nc.tensor.matmul(F[:, j * ROW + NS:(j + 1) * ROW],
                                                xt_sb[0:NV, k.slot(), j * P:(j + 1) * P],
                                                lin1_v_sb[:, :], start=True, stop=True)
                    last.then_inc(f_ready, 1)
                    pe.wait_ge(h_done, (k + 1).n)
                    wait(pe, prod_done, k.n)
                    for j in range(2):
                        last = nc.tensor.matmul(W[:, j, 0:NW], h_sb[j * NS:(j + 1) * NS, k.slot(), :],
                                                fc_w2_sb[j * NS:(j + 1) * NS, :], start=True, stop=True)
                    last.then_inc(w_ready, 1)
                a = k + 1
                if a.within(NPAIR):
                    wait(pe, e8_in[a.slot(UNROLL)], (a.round(UNROLL) + 1) * 16)
                    wait(pe, h_done, a.n)
                    for j in range(2):
                        last = nc.tensor.matmul(Z[j * NS:(j + 1) * NS, 0:P], fc_w1_sb[:, :],
                                                e8_sb[:, a.slot(UNROLL), j * P:(j + 1) * P], start=True, stop=True)
                    last.then_inc(z_ready, 1)
                    wait(pe, gathered[a.slot(UNROLL)], (a.round(UNROLL) + 1) * 32)
                    wait(pe, xt_copied, a.n)
                    for j in range(2):
                        nc.tensor.transpose(XT[:, j * P:(j + 1) * P], x_sb[:, a.slot(UNROLL), j, 0:P], ident_sb[:, :])
                        last = nc.tensor.transpose(XT[:, (2 + j) * P:(3 + j) * P], x_sb[:, a.slot(UNROLL), j, ROW - P:ROW], ident_sb[:, :])
                    last.then_inc(xt_ready, 1)

            software_pipeline(pe, -1, NPAIR + 3, 4, NPAIR - 2, step)

            pe.wait_ge(xt_copied, NPAIR)
            pe.wait_ge(pt_copied, NPAIR)
            pe.wait_ge(prod_done, NPAIR)
            pe.wait_ge(comb_copied, NPAIR)

            def node_step(k):
                a = k + 1
                if a.within(NG):
                    wait(pe, xn_in[a.slot(UNROLL)], (a.round(UNROLL) + 1) * 16)
                    wait(pe, xnt_copied, (a + -1).n)
                    wait(pe, xl_in[a.slot(UNROLL)], (a.round(UNROLL) + 1) * 16)
                    bank_a, bank_b = xnt_banks[a.slot()]
                    nc.tensor.transpose(bank_b[:, 0:P], xl_sb[:, a.slot(UNROLL), :], ident_sb[:, :])
                    for j in range(G):
                        last = nc.tensor.transpose(bank_a[:, j * P:(j + 1) * P], xn_sb[:, a.slot(UNROLL), j, 0:P], ident_sb[:, :])
                    last.then_inc(xnt_ready, 1)
                if k.within(NG):
                    pe.wait_ge(xnt_copied, (k + 1).n)
                    for j in range(G):
                        if k.i is not None or k.c > 0:
                            pe.wait_ge(y_chain, (k + -1).n * (2 * G) + (j + 1))
                        nc.tensor.matmul(sc_banks[j][:, 0:ROW], xnt_a_sb[:, k.slot(), j, :],
                                         sc_a_sb[:, :], start=True, stop=False)
                    for j in range(G):
                        r = j * (ROW - P)
                        last = nc.tensor.matmul(sc_banks[j][:, NV:ROW], xnt_b_sb[r:r + ROW - P, k.slot(), :],
                                                sc_b_sb[r:r + ROW - P, :], start=False, stop=True,
                                                )
                    last.then_inc(sc_ready, 1)

            software_pipeline(pe, -1, NG - 1, 1, NG - 2, node_step)

        @block.scalar
        def _(act):
            act.dma_start(dst_i[:, :], dst).then_inc(idx_in, 16)
            act.dma_start(ea4_sb[:, :, :], ea4).then_inc(idx_in, 16)

            def step(k):
                e = k + -4
                if e.within(NPAIR):
                    act.wait_ge(comb_ready, (e + 1).n)
                    for j in range(2):
                        wait(act, scattered[j], (e + (1 - UNROLL)).n * 16)
                    nc.scalar.copy(comb_sb[:, e.slot(UNROLL), :, :], COMB[:, 0:2 * ROWA].rearrange("p (j c) -> p j c", j=2)
                                   ).then_inc(comb_copied, 1)
                d = k + -2
                if d.within(NPAIR):
                    act.wait_ge(out_ready, (d + 1).n)
                    wait(act, comb_ready, (d + (1 - UNROLL)).n)
                    nc.scalar.copy(feat_sb[:, d.slot(UNROLL), :, :], OUT[:, 0:2 * OUTW].rearrange("p (j c) -> p j c", j=2)
                                   ).then_inc(out_copied, 1)
                c = k + -1
                if c.within(NPAIR):
                    act.wait_ge(prodt_ready, (c + 1).n)
                    wait(act, out_ready, (c + -1).n)
                    nc.scalar.copy(pt_sb[:, c.slot(), :], PT[:, :]).then_inc(pt_copied, 1)
                if k.within(NPAIR):
                    act.wait_ge(f_ready, (k + 1).n)
                    wait(act, prod_done, (k + -1).n)
                    nc.scalar.copy(f_sb[:, k.slot(), :, :], F[:, 0:2 * ROW].rearrange("p (j c) -> p j c", j=2)
                                   ).then_inc(f_copied, 1)
                a = k + 1
                if a.within(NPAIR):
                    act.wait_ge(z_ready, (a + 1).n)
                    wait(act, w_ready, (a + -1).n)
                    nc.scalar.activation(h_sb[:, a.slot(), :], Z[:, 0:P], ACT.Silu, scale=1.0 / math.sqrt(8.0)
                                         ).then_inc(h_done, 1)
                    act.wait_ge(xt_ready, (a + 1).n)
                    nc.scalar.copy(xt_sb[:, a.slot(), :], XT[:, :]).then_inc(xt_copied, 1)

            software_pipeline(act, -1, NPAIR + 3, 7, NPAIR - 2, step)
            act.wait_ge(prep, 3)

            def node_step(k):
                a = k + 1
                if a.within(NG):
                    act.wait_ge(red_done, (a + 1).n)
                    wait(act, triga_done, (a + -1).n)
                    nc.scalar.activation(redabs[:, a.slot(), :], red[:, a.slot(), :], ACT.Abs).then_inc(abs_done, 1)
                    nc.scalar.activation(trig[:, a.slot(), 1, :], red[:, a.slot(), :], ACT.Sin)
                    act.wait_ge(abs_done, (a + 1).n)
                    nc.scalar.activation(trig[:, a.slot(), 0, :], redabs[:, a.slot(), :], ACT.Sin,
                                         bias=half_pi[:, :], scale=-1.0).then_inc(trig_done, 1)
                    act.wait_ge(xnt_ready, (a + 1).n)
                    wait(act, sc_ready, (a + -1).n)
                    bank_a, bank_b = xnt_banks[a.slot()]
                    nc.scalar.copy(xnt_a_sb[:, a.slot(), :, :].rearrange("p j e -> p (j e)"), bank_a[:, :])
                    nc.scalar.copy(xnt_b_sb[:, a.slot(), :], bank_b[:, 0:P]).then_inc(xnt_copied, 1)
                s = k + -2
                if s.within(NG):
                    act.wait_ge(shift_done, (s + 1).n)
                    t = s.slot(UNROLL)
                    for j in range(G):
                        last = nc.scalar.activation(y_sb[:, t, j, :], y_sb[:, t, j, :], ACT.Identity,
                                                    bias=shift[:, t, j:j + 1], scale=rstd[:, t, j:j + 1])
                    last.then_inc(norm_done, 1)
                    act.wait_ge(norm_done, (s + 1).n)
                    act.dma_start(out_g[s.n, :, :], y_sb[:, t, :, :]).then_inc(stored[t], 16)

            software_pipeline(act, -1, NG + 1, 2, NG - 2, node_step)
            for s in range(UNROLL):
                act.wait_ge(stored[s], 16 * len(range(s, NG, UNROLL)))

        @block.vector
        def _(dve):
            dve.wait_ge(consts, 16 * N_CONSTS)
            s64, s32 = 1.0 / math.sqrt(NS), 1.0 / math.sqrt(MU)
            s96 = 1.0 / math.sqrt(NS + MU) / math.sqrt(NEIGHBORS)
            for w, s in ((fc_w2_sb, s64), (lin1_s_sb, s64), (lin1_v_sb, s32), (sc_a_sb[0:NV, :], s32), (sc_a_sb[NV:P, :], s64), (sc_b_sb, s64),
                         (lin2_a_sb, s96), (lin2_b_sb, s96)):
                last = nc.vector.tensor_scalar(w[:, :], w[:, :], s, None, ALU.mult)
            last.then_inc(ang_chain, 1)
            dve.wait_ge(ang_chain, 1)
            nc.vector.tensor_scalar(lin2_a_sb[0:NS, NS:NS + 1], lin2_a_sb[0:NS, NS:NS + 1], 0.1, None, ALU.mult)
            nc.vector.tensor_scalar(lin2_b_sb[NV:P, :], lin2_b_sb[NV:P, :], 1.0 / math.sqrt(3.0), None,
                                    ALU.mult).then_inc(ang_chain, 1)
            dve.wait_ge(ang_chain, 2)
            nc.vector.tensor_scalar(lin2_b_sb[NV:P, ROW:ROWA], lin2_b_sb[NV:P, ROW:ROWA], 0.1, None,
                                    ALU.mult).then_inc(weights_scaled, 1)
            dve.wait_ge(idx_in, 32)
            nc.vector.tensor_copy(dst_f[:, :], dst_i[:, :]).then_inc(ang_chain, 1)
            dve.wait_ge(ang_chain, 3)
            dve.wait_ge(prep, 3)
            nc.vector.tensor_tensor(to_spare[:, :], spare_row[:, :], dst_f[:, :], ALU.subtract).then_inc(ang_chain, 1)
            dve.wait_ge(ang_chain, 4)

            def step(k):
                d = k + -3
                if d.within(NPAIR):
                    o = feat_sb[:, d.slot(UNROLL), :, :]
                    dve.wait_ge(out_copied, (d + 1).n)
                    nc.vector.tensor_tensor(
                        vq_sb[:, :, :, :],
                        o[:, :, ROWA:OUTW].rearrange("p j (c o) -> p j c o", o=1).to_broadcast([P, 2, MU, 3]),
                        q_sb[:, d.slot(UNROLL), :, 1:4].rearrange("p j (o c) -> p j o c", o=1).to_broadcast([P, 2, MU, 3]),
                        ALU.mult).then_inc(vq_done, 1)
                    wait(dve, dstrow_in[d.slot(UNROLL)], (d.round(UNROLL) + 1) * 16)
                    wait(dve, comb_ready, (d + -1).n)
                    for j in range(2):
                        last = nc.vector.tensor_scalar(same_sb[:, d.slot(), 2 * j:2 + j, :], dstrow_sb[:, d.slot(UNROLL), j:2, :],
                                                       dst_f[:, bass.ds(d.n * 2 + j, 1)], None, ALU.is_equal)
                    last.then_inc(same_done, 1)
                    dve.wait_ge(vq_done, (d + 1).n)
                    nc.vector.tensor_tensor(o[:, :, 0:NV], o[:, :, 0:NV],
                                            vq_sb[:, :, :, :].rearrange("p j c o -> p j (c o)"),
                                            ALU.add).then_inc(feat_done, 1)
                    dve.wait_ge(same_done, (d + 1).n)
                    for j in range(2):
                        last = nc.vector.tensor_tensor_reduce(
                            out=junk_sb[:, 2 * j:2 + j, :].rearrange("p b e -> p (b e)"),
                            in0=same_sb[:, d.slot(), 2 * j:2 + j, :].rearrange("p b e -> p (b e)"),
                            in1=later_sb[:, 0:(2 - j) * P], scale=1.0,
                            scalar=0.0, op0=ALU.mult, op1=ALU.add, accum_out=later_cnt[:, d.slot(), j:j + 1])
                    last.then_inc(cnt_done, 1)
                if d.within(NPAIR):
                    dve.wait_ge(cnt_done, (d + 1).n)
                    nc.vector.scalar_tensor_tensor(shift_sb[:, d.slot(), :], later_cnt[:, d.slot(), :], 1.0,
                                                   to_spare[:, bass.ds(d.n * 2, 2)], ALU.min, ALU.mult
                                                   ).then_inc(spare_done, 1)
                if k.within(NPAIR):
                    wait(dve, gathered[k.slot(UNROLL)], (k.round(UNROLL) + 1) * 32)
                    nc.vector.tensor_tensor(q_sb[:, k.slot(UNROLL), :, :], ea4_sb[:, bass.ds(k.n * 2, 2), :],
                                            x_sb[:, k.slot(UNROLL), :, ROW:ROWA].to_broadcast([P, 2, 4]),
                                            ALU.mult).then_inc(q_done, 1)
                if d.within(NPAIR):
                    dve.wait_ge(spare_done, (d + 1).n)
                    for j in range(2):
                        wait(dve, scattered[j], (d + (1 - UNROLL)).n * 16)
                    nc.vector.tensor_tensor(row_sb[:, d.slot(UNROLL), :], shift_sb[:, d.slot(), :],
                                            dst_f[:, bass.ds(d.n * 2, 2)], ALU.add).then_inc(row_done, 1)
                if k.within(NPAIR):
                    f, q = f_sb[:, k.slot(), :, :], q_sb[:, k.slot(UNROLL), :, :]
                    w = W[:, :, 0:NW]
                    dve.wait_ge(q_done, (k + 1).n)
                    dve.wait_ge(f_copied, (k + 1).n)
                    nc.vector.tensor_tensor(tm_sb[:, :, :, :], f[:, :, NS:ROW].rearrange("p j (d c) -> p j d c", d=3),
                                            q[:, :, 1:4].rearrange("p j (d o) -> p j d o", o=1).to_broadcast([P, 2, 3, MU]),
                                            ALU.mult).then_inc(tm_done, 1)
                    dve.wait_ge(w_ready, (k + 1).n)
                    wait(dve, prodt_ready, (k + -1).n)
                    for j in range(2):
                        nc.vector.scalar_tensor_tensor(pa_sb[:, k.slot(), j, 0:NS], f[:, j, 0:NS], q[:, j, 0:1],
                                                       w[:, j, 0:NS], ALU.mult, ALU.mult)
                    dve.wait_ge(tm_done, (k + 1).n)
                    nc.vector.tensor_reduce(ts_sb[:, :, :], tm_sb[:, :, :, :].rearrange("p j d c -> p j c d"),
                                            mybir.AxisListType.X, ALU.add).then_inc(ts_done, 1)
                    for j in range(2):
                        nc.vector.scalar_tensor_tensor(
                            pb_sb[:, k.slot(), j, 0:NV].rearrange("p (d c) -> p d c", d=3),
                            f[:, j, NS:ROW].rearrange("p (d c) -> p d c", d=3), q[:, j, 0:1],
                            w[:, j, 2 * NS:2 * NS + MU].rearrange("p (o c) -> p o c", o=1).to_broadcast([P, 3, MU]),
                            ALU.mult, ALU.mult)
                    nc.vector.tensor_tensor(pa_sb[:, k.slot(), :, NS:P], f[:, :, 0:NS], w[:, :, NS:2 * NS], ALU.mult)
                    dve.wait_ge(ts_done, (k + 1).n)
                    nc.vector.tensor_tensor(pb_sb[:, k.slot(), :, NV:P], ts_sb[:, :, :], w[:, :, 2 * NS + MU:NW],
                                            ALU.mult).then_inc(prod_done, 1)

            software_pipeline(dve, 0, NPAIR + 2, 6, NPAIR - 1, step)

            C1, C2, C3 = 6.28125, 0.0019350051879882812, 3.019916050561733e-07
            MAGIC = 1.5 * 2.0 ** 23
            PI = 3.1415925
            LINKS = 6

            def angle(a):
                an, tu, t = ang[:, a.slot(), :], turns[:, a.slot(), :], a.slot(UNROLL)
                at = a.n * LINKS + 4
                wait(dve, acc_in[t], (a.round(UNROLL) + 1) * 16)
                wait(dve, xn_in[t], (a.round(UNROLL) + 1) * 16)
                nc.vector.tensor_tensor(an, cs_sb[:, t, :, ROW], xn_sb[:, t, :, ROW], ALU.mult).then_inc(ang_chain, 1)
                yield
                dve.wait_ge(ang_chain, at + 1)
                nc.vector.tensor_scalar(tu, an, 1.0 / (2.0 * math.pi), MAGIC, ALU.mult, ALU.add).then_inc(ang_chain, 1)
                yield
                dve.wait_ge(ang_chain, at + 2)
                nc.vector.tensor_scalar(tu, tu, MAGIC, None, ALU.subtract).then_inc(ang_chain, 1)
                yield
                for n, c in enumerate((C1, C2, C3)):
                    dve.wait_ge(ang_chain, at + 3 + n)
                    nc.vector.scalar_tensor_tensor(an, tu, -c, an, ALU.mult, ALU.add).then_inc(ang_chain, 1)
                    yield
                dve.wait_ge(ang_chain, at + 6)
                wait(dve, trig_done, (a + -1).n)
                nc.vector.tensor_scalar(red[:, a.slot(), :], an, -PI, PI, ALU.max, ALU.min).then_inc(red_done, 1)
                yield

            def node_step(k):
                a = k + 2
                links = angle(a) if a.within(NG) else iter(())
                if k.within(NG):
                    t = k.slot(UNROLL)
                    ta = trig_a[:, k.slot(), :, :]
                    dve.wait_ge(triga_done, (k + 1).n)
                    dve.wait_ge(sc_ready, (k + 1).n)
                    wait(dve, stored[t], k.round(UNROLL) * 16)
                    for j in range(G):
                        nc.vector.scalar_tensor_tensor(y_sb[:, t, j, :], sc_banks[j][:, 0:ROW],
                                                       ta[:, 0, j:j + 1], xn_sb[:, t, j, 0:ROW],
                                                       ALU.mult, ALU.add).then_inc(y_chain, 1)
                        next(links, None)
                    for j in range(G):
                        dve.wait_ge(y_chain, k.n * 2 * G + (j + 1))
                        nc.vector.scalar_tensor_tensor(y_sb[:, t, j, :], cs_sb[:, t, j, 0:ROW],
                                                       ta[:, 1, j:j + 1], y_sb[:, t, j, :],
                                                       ALU.mult, ALU.add).then_inc(y_chain, 1)
                        next(links, None)
                    for j in range(G):
                        dve.wait_ge(y_chain, k.n * 2 * G + G + (j + 1))
                        nc.vector.bn_stats(stats[:, j, :], y_sb[:, t, j, :]).then_inc(stat_chain, 1)
                    for j in range(G):
                        dve.wait_ge(stat_chain, k.n * G + (j + 1))
                        dve.sem_inc(dve_passed, 1)
                        last = nc.vector.bn_aggr(meanvar[:, t, j, :], stats[:, j, :])
                    last.then_inc(mv_done, 1)
                for _ in links:
                    pass
                b = k + 1
                if b.within(NG):
                    dve.wait_ge(trig_done, (b + 1).n)
                    attr = xn_sb[:, b.slot(UNROLL), :, ROW:ROWA].rearrange("p g o -> p o g")
                    nc.vector.tensor_tensor(trig_a[:, b.slot(), :, :], trig[:, b.slot(), :, :],
                                            attr.to_broadcast([P, 2, G]), ALU.mult).then_inc(triga_done, 1)

            software_pipeline(dve, -2, NG - 1, UNROLL, NG - 3, node_step)


def layouts(x, src, dst, edge_attr_4, edge_attr_8, node_vec1, sc_w0, sc_w1, lin1_w0, lin1_w1, fc_w1,
            fc_w2, lin2_w0, lin2_w1, lin3_w, tiles):
    n, e = x.shape[0], src.shape[0]
    rows = tiles * P
    f32 = np.float32
    xa = np.zeros((rows, ROWA), f32)
    xa[:n, :NV], xa[:n, NV:ROW], xa[:n, ROW] = x[:, NS:], x[:, :NS], node_vec1[:, 0]
    src_p = np.zeros(rows, np.int32)
    src_p[:e] = src
    dst_p = np.full(rows, n, np.int32)
    dst_p[:e] = dst
    ea4 = np.zeros((rows, 4), f32)
    ea4[:e] = edge_attr_4
    ea8 = np.zeros((rows, 8), f32)
    ea8[:e] = edge_attr_8

    def by_component(w, rows_grouped, cols_grouped):
        u, c = w.shape
        m = np.zeros((u, 3, c, 3), f32)
        for d in range(3):
            m[:, d, :, d] = w
        if rows_grouped:
            m = m.transpose(1, 0, 2, 3).reshape(3 * u, c, 3)
        else:
            m = m.reshape(3 * u, c, 3)
        if cols_grouped:
            m = m.transpose(0, 2, 1)
        return np.ascontiguousarray(m.reshape(3 * u, 3 * c))

    lin2_a = np.zeros((P, NS + 1 + MU), f32)
    lin2_a[:NS, :NS] = lin2_w0[:NS]
    lin2_a[:NS, NS] = lin3_w[:NS, 0]
    lin2_a[NS:, NS + 1:] = lin2_w1[:NS]
    lin2_b = np.zeros((P, OUTW), f32)
    lin2_b[:NV, :NV] = by_component(lin2_w1[NS:], True, False)
    lin2_b[NV:, NV:ROW] = lin2_w0[NS:]
    lin2_b[NV:, ROW] = lin3_w[NS:, 0]
    sc_a = np.zeros((P, ROW), f32)
    sc_a[:NV, :NV] = by_component(sc_w1, False, False)
    sc_a[NV:, NV:] = sc_w0[:P - NV]
    order = np.arange(P)
    return {
        "xa": xa,
        "x_last": np.ascontiguousarray(xa[:, P:ROW].reshape(tiles // G, P, G * (ROW - P))),
        "src": np.ascontiguousarray(src_p.reshape(P, tiles // 2, 2).transpose(1, 0, 2)),
        "dst": dst_p.reshape(P, tiles),
        "dst_rows": np.ascontiguousarray(dst_p.reshape(P, tiles).T).reshape(tiles // 2, 2, P),
        "ea4": ea4.reshape(P, tiles, 4),
        "ea8t": np.ascontiguousarray(ea8.reshape(P, tiles // 2, 2, 8).transpose(1, 3, 2, 0)).reshape(tiles // 2, 8, 2 * P),
        "fc_w1": np.asarray(fc_w1),
        "fc_w2": np.concatenate([fc_w2, fc_w2]),
        "lin1_s": np.concatenate([lin1_w0, lin1_w0]),
        "lin1_v": by_component(lin1_w1, False, True),
        "lin2_a": lin2_a,
        "lin2_b": lin2_b,
        "sc_a": sc_a,
        "sc_b": np.concatenate([sc_w0[P - NV:]] * G),
        "ident": np.eye(P, dtype=f32),
        "later": (np.arange(2 * P)[None, :] > order[:, None]).astype(f32),
    }


def kernel(x, src, dst, edge_attr_4, edge_attr_8, node_vec1, L0_gnn_sc_w0, L0_gnn_sc_w1, L0_gnn_lin1_w0,
           L0_gnn_lin1_w1, L0_gnn_fc_w1, L0_gnn_fc_w2, L0_gnn_lin2_w0, L0_gnn_lin2_w1, L0_gnn_lin3_w):
    import concourse.bacc as bacc
    from concourse.bass_utils import run_bass_kernel_spmd

    n = x.shape[0]
    tiles = -(-max(n + 1, src.shape[0]) // (P * 2 * G)) * 2 * G
    arrays = layouts(*(np.asarray(a) for a in (
        x, src, dst, edge_attr_4, edge_attr_8, node_vec1, L0_gnn_sc_w0, L0_gnn_sc_w1, L0_gnn_lin1_w0,
        L0_gnn_lin1_w1, L0_gnn_fc_w1, L0_gnn_fc_w2, L0_gnn_lin2_w0, L0_gnn_lin2_w1, L0_gnn_lin3_w)), tiles)
    nc = bacc.Bacc("TRN2", target_bir_lowering=False, num_devices=1)
    args = {k: nc.dram_tensor(k, a.shape, mybir.dt.from_np(a.dtype), kind="ExternalInput").ap()
            for k, a in arrays.items()}
    args["acc"] = nc.dram_tensor("acc", [(tiles + SPARE) * P, ROWA], mybir.dt.float32, kind="Internal").ap()
    args["out"] = nc.dram_tensor("out", [tiles * P, ROW], mybir.dt.float32, kind="ExternalOutput").ap()
    gnn_program(nc, **args)
    r = run_bass_kernel_spmd(nc, [arrays], core_ids=[0])
    got = r.results[0]["out"][:n]
    return np.concatenate([got[:, NV:], got[:, :NV]], axis=1)
```

```python
import concourse.bass as bass
from concourse import mybir
from contextlib import ExitStack
import math
import numpy as np

P = 128
NS, NV, MU = 64, 96, 32
ROW = NS + NV
ROWA = ROW + 1
NW = 2 * NS + 2 * MU
EDGE_S = 8
OUTW = ROWA + MU
G = 4
SPARE = 8
RING = 24
AHEAD = 20
CATCH_UP = 3
ZEROS_EACH = 3
ZEROING = 3
STORE_LAG = 6
EPS = 1e-5
NEIGHBORS = 16.0

CONSTANTS = {
    "ident": (P, P), "later": (P, 2 * P), "fc_w1": (2 * EDGE_S, 2 * NS), "fc_w2": (P, NW), "lin1_a": (P, ROW),
    "lin1_b": (NS, 2 * NS), "lin2_a": (P, NS + 1 + MU), "lin2_b": (P, OUTW), "sc_a": (P, ROW), "sc_b": (P, 2 * NS),
}

UNROLL = 4


class Step:

    def __init__(self, i, c, each=UNROLL):
        self.i, self.c, self.each = i, c, each
        self.n = c if i is None else i * each + c

    def __add__(self, d):
        return Step(self.i, self.c + d, self.each)

    def slot(self, slots=2):
        return self.c % slots

    def round(self, slots=2):
        return self.c // slots if self.i is None else self.i * (self.each // slots) + self.c // slots

    def within(self, count):
        return self.i is not None or 0 <= self.c < count


def wait(eng, sem, count):
    if not isinstance(count, int) or count > 0:
        eng.wait_ge(sem, count)


def software_pipeline(eng, first, last, fill, drain, step, each=UNROLL):
    count = max(drain - fill + 1, 0) // each
    for k in range(first, fill):
        step(Step(None, k))
    if count:
        with eng.Fori(0, count, 1) as i:
            for u in range(each):
                step(Step(i, fill + u, each))
    for k in range(fill + each * count, last + 1):
        step(Step(None, k))


def gnn_program(nc, xa, x_odd, x_last, src, dst, dst_rows, ea4, ea8t, constants, acc, out):
    fp32, i32 = mybir.dt.float32, mybir.dt.int32
    ALU, ACT = mybir.AluOpType, mybir.ActivationFunctionType
    NT = dst.shape[1]
    NPAIR = NT // 2
    NG = NT // G
    NODES = NT * P
    xa_g = xa.rearrange("(g p j) c -> g p (j c)", p=P, j=G)
    out_g = out.rearrange("(g p j) c -> g p (j c)", p=P, j=G)
    ZEROS = acc.shape[0] // (SPARE * P)
    acc_z = acc.rearrange("(c p k) r -> c p (k r)", p=P, k=SPARE)
    acc_g = acc[0:NODES, :].rearrange("(g p j) c -> g p (j c)", p=P, j=G)

    with ExitStack() as ctx:
        def sb(name, shape, dt=fp32):
            return ctx.enter_context(nc.sbuf_tensor(name, shape, dt))

        def ps(name):
            return ctx.enter_context(nc.psum_tensor(name, [P, 512], fp32))

        def sem(name):
            return ctx.enter_context(nc.semaphore(name))

        constants_sb = sb("constants_sb", [P, constants.shape[1]])
        views, column = [], 0
        for rows, columns in CONSTANTS.values():
            views.append(constants_sb[0:rows, column:column + columns])
            column += columns
        ident_sb, later_sb, fc_w1_sb, fc_w2_sb, lin1_a_sb, lin1_b_sb, lin2_a_sb, lin2_b_sb, sc_a_sb, sc_b_sb = views
        half_pi = sb("half_pi", [P, 1])
        minus_half = sb("minus_half", [P, G])
        dst_i = sb("dst_i", [P, NT], i32)
        dst_f = sb("dst_f", [P, NT])
        spare_row = sb("spare_row", [P, NT], i32)
        to_spare = sb("to_spare", [P, NT])
        ea4_sb = sb("ea4_sb", [P, NT, 4])
        zeros = sb("zeros", [P, SPARE * ROWA])
        src_sb = sb("src_sb", [P, UNROLL, 2], i32)
        x_sb = sb("x_sb", [P, UNROLL, 2 * ROWA])
        e8_sb = sb("e8_sb", [2 * EDGE_S, UNROLL, P])
        dstrow_sb = sb("dstrow_sb", [P, UNROLL, 2, P], i32)
        xt_sb = sb("xt_sb", [P, 2, 3 * P])
        h_sb = sb("h_sb", [P, 2, P])
        f_sb = sb("f_sb", [P, 2, 2, ROW])
        q_sb = sb("q_sb", [P, UNROLL, 2, 4])
        tm_sb = sb("tm_sb", [P, 2, 3, MU])
        ts_sb = sb("ts_sb", [P, 2, MU])
        pa_sb = sb("pa_sb", [P, 2, 2, P])
        pb_sb = sb("pb_sb", [P, 2, 2, P])
        pt_sb = sb("pt_sb", [P, 2, 4 * P])
        vq_sb = sb("vq_sb", [P, 2, MU, 3])
        feat_sb = sb("feat_sb", [P, UNROLL, 2, OUTW])
        same_sb = sb("same_sb", [P, 2, 3, P])
        junk_sb = sb("junk_sb", [P, 3, P])
        later_cnt = sb("later_cnt", [P, 2, 2])
        shift_sb = sb("shift_sb", [P, 2, 2])
        row_sb = sb("row_sb", [P, RING, 2], i32)
        comb_sb = sb("comb_sb", [P, RING, 2, ROWA])
        xn_sb = sb("xn_sb", [P, UNROLL, G, ROWA])
        cs_sb = sb("cs_sb", [P, UNROLL, G, ROWA])
        xl_sb = sb("xl_sb", [P, UNROLL, P])
        xnt_a_sb = sb("xnt_a_sb", [P, 2, G, P])
        xnt_b_sb = sb("xnt_b_sb", [P, 2, P])
        y_sb = sb("y_sb", [P, UNROLL, G, ROW])
        ang = sb("ang", [P, 2, G])
        turns = sb("turns", [P, 2, G])
        red = sb("red", [P, 2, G])
        redabs = sb("redabs", [P, 2, G])
        trig = sb("trig", [P, 2, 2, G])
        trig_a = sb("trig_a", [P, 2, 2, G])
        stats = sb("stats", [P, G, 6])
        meanvar = sb("meanvar", [P, UNROLL, G, 2])
        vareps = sb("vareps", [P, G])
        rstd = sb("rstd", [P, UNROLL, G])
        shift = sb("shift", [P, UNROLL, G])
        XT, Z, F, PT, OUT, COMB = (ps(n) for n in ("XT", "Z", "F", "PT", "OUT", "COMB"))
        W = ctx.enter_context(nc.psum_tensor("W", [P, 2, 512], fp32))

        xnt_banks = ((XT, PT), (F, Z))
        sc_banks = ((W[:, 0, :], W[:, 1, :]), (OUT, COMB))

        consts = sem("consts")
        idx_in = sem("idx_in")
        zeroed_tile = sem("zeroed_tile")
        acc_zeroed = [sem(f"acc_zeroed{s}") for s in range(ZEROING)]
        prep = sem("prep")
        weights_scaled = sem("weights_scaled")
        gathered = [sem(f"gathered{s}") for s in range(UNROLL)]
        src_in = [sem(f"src_in{s}") for s in range(UNROLL)]
        e8_in = [sem(f"e8_in{s}") for s in range(UNROLL)]
        dstrow_in = [sem(f"dstrow_in{s}") for s in range(UNROLL)]
        scattered = [sem(f"scattered{j}") for j in range(2)]
        xt_ready, z_ready, f_ready, w_ready = sem("xt_ready"), sem("z_ready"), sem("f_ready"), sem("w_ready")
        prodt_ready, out_ready, comb_ready = sem("prodt_ready"), sem("out_ready"), sem("comb_ready")
        h_done, xt_copied, f_copied, pt_copied = sem("h_done"), sem("xt_copied"), sem("f_copied"), sem("pt_copied")
        out_copied, comb_copied = sem("out_copied"), sem("comb_copied")
        q_done, prod_done, feat_done = sem("q_done"), sem("prod_done"), sem("feat_done")
        same_done, row_done = sem("same_done"), sem("row_done")
        tm_done, ts_done, vq_done, cnt_done, spare_done = (sem(n) for n in ("tm_done", "ts_done", "vq_done", "cnt_done", "spare_done"))
        xn_in = [sem(f"xn_in{s}") for s in range(UNROLL)]
        xl_in = [sem(f"xl_in{s}") for s in range(UNROLL)]
        acc_in = [sem(f"acc_in{s}") for s in range(UNROLL)]
        stored = [sem(f"stored{s}") for s in range(UNROLL)]
        xnt_ready, xnt_copied, sc_ready = sem("xnt_ready"), sem("xnt_copied"), sem("sc_ready")
        red_done, abs_done, trig_done = sem("red_done"), sem("abs_done"), sem("trig_done")
        mv_done, eps_done, rstd_done, norm_done = (sem(n) for n in ("mv_done", "eps_done", "rstd_done", "norm_done"))
        comb_free = sem("comb_free")
        pool_passed, dve_passed, sp_passed = sem("pool_passed"), sem("dve_passed"), sem("sp_passed")
        chain = sem("chain")
        y_started = sem("y_started")
        y_done = sem("y_done")
        sc_scaled = sem("sc_scaled")
        conv_times_sine = sem("conv_times_sine")
        conv_scaled = sem("conv_scaled")
        stats_done = sem("stats_done")
        triga_done = sem("triga_done")
        shift_done = sem("shift_done")
        block = ctx.enter_context(nc.Block())

        @block.sync
        def _(sp):
            sp.dma_start(constants_sb[:, :], constants).then_inc(consts, 16)

            def zero(c):
                wait(sp, acc_zeroed[c.slot(ZEROING)], c.round(ZEROING) * 16)
                sp.sem_inc(sp_passed, 1)
                sp.dma_start(acc_z[c.n, :, :], zeros[:, :]).then_inc(acc_zeroed[c.slot(ZEROING)], 16)

            def load(k):
                if k.within(NPAIR):
                    wait(sp, gathered[k.slot(UNROLL)], k.round(UNROLL) * 32)
                    sp.sem_inc(sp_passed, 1)
                    sp.dma_start(src_sb[:, k.slot(UNROLL), :], src[k.n, :, :]).then_inc(src_in[k.slot(UNROLL)], 16)
                    wait(sp, z_ready, (k + (1 - UNROLL)).n)
                    sp.sem_inc(sp_passed, 1)
                    sp.dma_start(e8_sb[:, k.slot(UNROLL), :], ea8t[k.n, :, :]).then_inc(e8_in[k.slot(UNROLL)], 16)
                d = k + -2
                if d.within(NPAIR):
                    wait(sp, same_done, (d + (1 - UNROLL)).n)
                    sp.sem_inc(sp_passed, 1)
                    sp.dma_start(dstrow_sb[:, d.slot(UNROLL), :, :],
                                 dst_rows[d.n, :, :].rearrange("(o j) e -> o j e", o=1).to_broadcast([P, 2, P])
                                 ).then_inc(dstrow_in[d.slot(UNROLL)], 16)

            def load_and_zero(k, c):
                load(k)
                for n in range(ZEROS_EACH):
                    zero(c + n)

            bodies = min(ZEROS // (UNROLL * ZEROS_EACH), NPAIR // UNROLL - 1)
            c0 = ZEROS - bodies * UNROLL * ZEROS_EACH
            for k in range(UNROLL):
                load(Step(None, k))
            sp.wait_ge(zeroed_tile, 1)
            for c in range(c0):
                zero(Step(None, c))
            if bodies:
                for u in range(UNROLL):
                    load_and_zero(Step(None, UNROLL + u), Step(None, c0 + ZEROS_EACH * u))
            if bodies > 1:
                with sp.Fori(1, bodies, 1) as i:
                    for u in range(UNROLL):
                        load_and_zero(Step(i, UNROLL + u), Step(i, c0 + ZEROS_EACH * u, UNROLL * ZEROS_EACH))
            k0 = UNROLL * (1 + bodies)
            software_pipeline(sp, k0, NPAIR + 1, max(k0, 2 * UNROLL), NPAIR - 1, load)

            def load_and_store(g):
                if g.within(NG):
                    wait(sp, y_done, (g + (1 - UNROLL)).n)
                    sp.sem_inc(sp_passed, 1)
                    sp.dma_start(xn_sb[:, g.slot(UNROLL), :, :], xa_g[g.n, :, :]).then_inc(xn_in[g.slot(UNROLL)], 16)
                    sp.dma_start(xl_sb[:, g.slot(UNROLL), :], x_last[g.n, :, :]).then_inc(xl_in[g.slot(UNROLL)], 16)
                    if g.i is None and g.c == 0:
                        for j in range(2):
                            sp.wait_ge(scattered[j], 16 * NPAIR)
                    sp.dma_start(cs_sb[:, g.slot(UNROLL), :, :], acc_g[g.n, :, :]).then_inc(acc_in[g.slot(UNROLL)], 16)
                s = g + -STORE_LAG
                if s.within(NG):
                    sp.wait_ge(norm_done, (s + 1).n)
                    sp.dma_start(out_g[s.n, :, :], y_sb[:, s.slot(UNROLL), :, :]).then_inc(stored[s.slot(UNROLL)], 16)

            software_pipeline(sp, 0, NG - 1 + STORE_LAG, STORE_LAG, NG - 1, load_and_store)
            for s in range(UNROLL):
                sp.wait_ge(stored[s], 16 * len(range(s, NG, UNROLL)))

        @block.gpsimd
        def _(pool):
            pool.memset(zeros[:, :], 0.0).then_inc(zeroed_tile, 1)
            pool.memset(half_pi[:, :], math.pi / 2).then_inc(prep, 1)
            pool.memset(minus_half[:, :], -0.5).then_inc(prep, 1)
            pool.iota(spare_row[:, :], pattern=[[0, NPAIR], [P, 2]], base=NODES, channel_multiplier=1).then_inc(prep, 1)

            pool.sem_inc(comb_free, RING)

            def gather(g):
                wait(pool, xt_ready, (g + (1 - UNROLL)).n)
                wait(pool, q_done, (g + (1 - UNROLL)).n)
                wait(pool, src_in[g.slot(UNROLL)], (g.round(UNROLL) + 1) * 16)
                pool.sem_inc(pool_passed, 1)
                for j, table in enumerate((xa, x_odd)):
                    pool.indirect_dma_start(
                        out=x_sb[:, g.slot(UNROLL), j * ROWA:(j + 1) * ROWA], out_offset=None, in_=table,
                        in_offset=bass.IndirectOffsetOnAxis(ap=src_sb[:, g.slot(UNROLL), j:j + 1], axis=0),
                    ).then_inc(gathered[g.slot(UNROLL)], 16)

            def scatter(n, slot):
                pool.wait_ge(row_done, n + 1)
                pool.wait_ge(comb_copied, n + 1)
                for j in range(2):
                    wait(pool, scattered[j], n * 16)
                if not isinstance(n, int) or n > 0:
                    pool.sem_inc(comb_free, 1)
                for j in range(2):
                    pool.indirect_dma_start(
                        out=acc, out_offset=bass.IndirectOffsetOnAxis(ap=row_sb[:, slot, j:j + 1], axis=0),
                        in_=comb_sb[:, slot, j, :], in_offset=None, compute_op=ALU.add,
                    ).then_inc(scattered[j], 16)

            ahead = min(AHEAD, NPAIR)
            software_pipeline(pool, 0, ahead - 1, UNROLL, ahead - 1, gather)
            for s in range(ZEROING):
                pool.wait_ge(acc_zeroed[s], 16 * len(range(s, ZEROS, ZEROING)))
            scatter(0, 0)

            def bodies(g0, s0, gathers, count):
                if count > 0:
                    with pool.Fori(0, count, 1) as i:
                        for u in range(RING):
                            if u * gathers // RING < (u + 1) * gathers // RING:
                                g = u * gathers // RING
                                gather(Step(i, g0 + g, gathers))
                            scatter(i * RING + (s0 + u), (s0 + u) % RING)

            fewer = RING - UNROLL
            catch_up = min(CATCH_UP, (NPAIR - ahead) // fewer)
            bodies(ahead, 1, fewer, catch_up)
            g0, s0 = ahead + catch_up * fewer, 1 + catch_up * RING
            even = (NPAIR - g0) // RING
            bodies(g0, s0, RING, even)
            for g in range(g0 + even * RING, NPAIR):
                gather(Step(None, g))
                scatter(g - g0 + s0, (g - g0 + s0) % RING)
            for n in range(s0 + NPAIR - g0, NPAIR):
                scatter(n, n % RING)

            def node_step(k):
                r = k + -1
                if r.within(NG):
                    pool.wait_ge(eps_done, (r + 1).n)
                    wait(pool, norm_done, (r + (1 - UNROLL)).n)
                    pool.sem_inc(pool_passed, 1)
                    pool.tensor_tensor(out=rstd[:, r.slot(UNROLL), :], in0=vareps[:, :], in1=minus_half[:, :],
                                       op=ALU.pow).then_inc(rstd_done, 1)
                b = k + 1
                if b.within(NG):
                    pool.wait_ge(triga_done, (b + 1).n)
                    cs = cs_sb[:, b.slot(UNROLL), :, 0:ROW]
                    sine = trig_a[:, b.slot(), 1, :].rearrange("p (g o) -> p g o", o=1).to_broadcast([P, G, ROW])
                    pool.tensor_tensor(out=cs, in0=cs, in1=sine, op=ALU.mult).then_inc(conv_times_sine, 1)
                    pool.wait_ge(conv_times_sine, (b + 1).n)
                    half = cs_sb[:, b.slot(UNROLL), G // 2:G, 0:ROW]
                    pool.tensor_tensor(out=half, in0=half, in1=xn_sb[:, b.slot(UNROLL), G // 2:G, 1:ROWA],
                                       op=ALU.add).then_inc(conv_scaled, 1)

            software_pipeline(pool, -1, NG, UNROLL, NG - 3, node_step)

        @block.tensor
        def _(pe):
            pe.wait_ge(consts, 16)
            pe.wait_ge(weights_scaled, 1)

            def step(k):
                e = k + -4
                if e.within(NPAIR):
                    pe.wait_ge(feat_done, (e + 1).n)
                    pe.wait_ge(same_done, (e + 1).n)
                    wait(pe, comb_copied, e.n)
                    for j, b, f, start in ((0, 0, 0, True), (1, 1, 0, True), (1, 2, 1, False)):
                        last = nc.tensor.matmul(COMB[:, j * ROWA:(j + 1) * ROWA], same_sb[:, e.slot(), b, :],
                                                feat_sb[:, e.slot(UNROLL), f, 0:ROWA], start=start, stop=j == 0 or not start)
                    last.then_inc(comb_ready, 1)
                d = k + -2
                if d.within(NPAIR):
                    pe.wait_ge(pt_copied, (d + 1).n)
                    wait(pe, out_copied, d.n)
                    for j in range(2):
                        o = j * OUTW
                        nc.tensor.matmul(OUT[:, o:o + OUTW], pt_sb[:, d.slot(), (2 + j) * P:(3 + j) * P],
                                         lin2_b_sb[:, :], start=True, stop=False)
                        last = nc.tensor.matmul(OUT[:, o + NV:o + OUTW], pt_sb[:, d.slot(), j * P:(j + 1) * P],
                                                lin2_a_sb[:, :], start=False, stop=True)
                    last.then_inc(out_ready, 1)
                c = k + -1
                if c.within(NPAIR):
                    pe.wait_ge(prod_done, (c + 1).n)
                    wait(pe, pt_copied, c.n)
                    for j in range(2):
                        nc.tensor.transpose(PT[:, j * P:(j + 1) * P], pa_sb[:, c.slot(), j, :], ident_sb[:, :])
                    for j in range(2):
                        last = nc.tensor.transpose(PT[:, (2 + j) * P:(3 + j) * P], pb_sb[:, c.slot(), j, :], ident_sb[:, :])
                    last.then_inc(prodt_ready, 1)
                if k.within(NPAIR):
                    pe.wait_ge(xt_copied, (k + 1).n)
                    wait(pe, f_copied, k.n)
                    for j in range(2):
                        nc.tensor.matmul(F[:, j * ROW:(j + 1) * ROW], xt_sb[:, k.slot(), j * P:(j + 1) * P],
                                         lin1_a_sb[:, :], start=j == 0, stop=False)
                    last = nc.tensor.matmul(F[:, 0:2 * ROW].rearrange("p (j c) -> p j c", j=2)[:, :, 0:NS],
                                            xt_sb[0:NS, k.slot(), 2 * P:3 * P],
                                            lin1_b_sb[:, :].rearrange("p (j c) -> p j c", j=2), start=False, stop=True)
                    last.then_inc(f_ready, 1)
                    pe.wait_ge(h_done, (k + 1).n)
                    wait(pe, prod_done, k.n)
                    for j in range(2):
                        last = nc.tensor.matmul(W[:, j, 0:NW], h_sb[j * NS:(j + 1) * NS, k.slot(), :],
                                                fc_w2_sb[j * NS:(j + 1) * NS, :], start=True, stop=True)
                    last.then_inc(w_ready, 1)
                a = k + 1
                if a.within(NPAIR):
                    wait(pe, e8_in[a.slot(UNROLL)], (a.round(UNROLL) + 1) * 16)
                    wait(pe, h_done, a.n)
                    nc.tensor.matmul(Z[:, 0:P], fc_w1_sb[:, :], e8_sb[:, a.slot(UNROLL), :],
                                     start=True, stop=True).then_inc(z_ready, 1)
                    wait(pe, gathered[a.slot(UNROLL)], (a.round(UNROLL) + 1) * 32)
                    wait(pe, xt_copied, a.n)
                    for b, column in enumerate((1, ROWA + ROW - P, 1 + P)):
                        last = nc.tensor.transpose(XT[:, b * P:(b + 1) * P], x_sb[:, a.slot(UNROLL), column:column + P],
                                                   ident_sb[:, :])
                    last.then_inc(xt_ready, 1)

            software_pipeline(pe, -1, NPAIR + 3, 4, NPAIR - 2, step)

            pe.wait_ge(xt_copied, NPAIR)
            pe.wait_ge(pt_copied, NPAIR)
            pe.wait_ge(prod_done, NPAIR)
            pe.wait_ge(comb_copied, NPAIR)

            def node_step(k):
                a = k + 1
                if a.within(NG):
                    wait(pe, xn_in[a.slot(UNROLL)], (a.round(UNROLL) + 1) * 16)
                    wait(pe, xnt_copied, (a + -1).n)
                    wait(pe, xl_in[a.slot(UNROLL)], (a.round(UNROLL) + 1) * 16)
                    bank_a, bank_b = xnt_banks[a.slot()]
                    nc.tensor.transpose(bank_b[:, 0:P], xl_sb[:, a.slot(UNROLL), :], ident_sb[:, :])
                    for j in range(G):
                        last = nc.tensor.transpose(bank_a[:, j * P:(j + 1) * P], xn_sb[:, a.slot(UNROLL), j, 1:1 + P], ident_sb[:, :])
                    last.then_inc(xnt_ready, 1)
                if k.within(NG):
                    pe.wait_ge(xnt_copied, (k + 1).n)
                    wait(pe, y_started, (k + -1).n * (G // 2))
                    wait(pe, sc_scaled, (k + -1).n)
                    banks = sc_banks[k.slot()]
                    for b in range(2):
                        for j in range(2):
                            nc.tensor.matmul(banks[b][:, j * ROW:(j + 1) * ROW], xnt_a_sb[:, k.slot(), 2 * b + j, :],
                                             sc_a_sb[:, :], start=j == 0, stop=False)
                    for b in range(2):
                        r = b * NS
                        last = nc.tensor.matmul(banks[b][:, 0:2 * ROW].rearrange("p (j c) -> p j c", j=2)[:, :, NV:ROW],
                                                xnt_b_sb[r:r + NS, k.slot(), :],
                                                sc_b_sb[r:r + NS, :].rearrange("p (j c) -> p j c", j=2),
                                                start=False, stop=True)
                    last.then_inc(sc_ready, 1)

            software_pipeline(pe, -1, NG - 1, 1, NG - 2, node_step)

        @block.scalar
        def _(act):
            act.dma_start(dst_i[:, :], dst).then_inc(idx_in, 16)
            act.dma_start(ea4_sb[:, :, :], ea4).then_inc(idx_in, 16)

            def step(k):
                e = k + -4
                if e.within(NPAIR):
                    act.wait_ge(comb_ready, (e + 1).n)
                    act.wait_ge(comb_free, (e + 1).n)
                    nc.scalar.copy(comb_sb[:, e.n % RING, :, :], COMB[:, 0:2 * ROWA].rearrange("p (j c) -> p j c", j=2)
                                   ).then_inc(comb_copied, 1)
                d = k + -2
                if d.within(NPAIR):
                    act.wait_ge(out_ready, (d + 1).n)
                    wait(act, comb_ready, (d + (1 - UNROLL)).n)
                    nc.scalar.copy(feat_sb[:, d.slot(UNROLL), :, :], OUT[:, 0:2 * OUTW].rearrange("p (j c) -> p j c", j=2)
                                   ).then_inc(out_copied, 1)
                c = k + -1
                if c.within(NPAIR):
                    act.wait_ge(prodt_ready, (c + 1).n)
                    wait(act, out_ready, (c + -1).n)
                    nc.scalar.copy(pt_sb[:, c.slot(), :], PT[:, :]).then_inc(pt_copied, 1)
                if k.within(NPAIR):
                    act.wait_ge(f_ready, (k + 1).n)
                    wait(act, prod_done, (k + -1).n)
                    nc.scalar.copy(f_sb[:, k.slot(), :, :], F[:, 0:2 * ROW].rearrange("p (j c) -> p j c", j=2)
                                   ).then_inc(f_copied, 1)
                a = k + 1
                if a.within(NPAIR):
                    act.wait_ge(z_ready, (a + 1).n)
                    wait(act, w_ready, (a + -1).n)
                    nc.scalar.activation(h_sb[:, a.slot(), :], Z[:, 0:P], ACT.Silu, scale=1.0 / math.sqrt(8.0)
                                         ).then_inc(h_done, 1)
                    act.wait_ge(xt_ready, (a + 1).n)
                    nc.scalar.copy(xt_sb[:, a.slot(), :], XT[:, 0:3 * P]).then_inc(xt_copied, 1)

            software_pipeline(act, -1, NPAIR + 3, 7, NPAIR - 2, step)
            act.wait_ge(prep, 3)

            def node_step(k):
                a = k + 1
                if a.within(NG):
                    act.wait_ge(xnt_ready, (a + 1).n)
                    wait(act, sc_ready, (a + -1).n)
                    bank_a, bank_b = xnt_banks[a.slot()]
                    nc.scalar.copy(xnt_a_sb[:, a.slot(), :, :].rearrange("p j e -> p (j e)"), bank_a[:, :])
                    nc.scalar.copy(xnt_b_sb[:, a.slot(), :], bank_b[:, 0:P]).then_inc(xnt_copied, 1)
                if k.within(NG):
                    act.wait_ge(sc_ready, (k + 1).n)
                    act.wait_ge(triga_done, (k + 1).n)
                    wait(act, stored[k.slot(UNROLL)], k.round(UNROLL) * 16)
                    for j in range(G // 2, G):
                        last = nc.scalar.activation(y_sb[:, k.slot(UNROLL), j, :],
                                                    sc_banks[k.slot()][1][:, (j - G // 2) * ROW:(j - G // 2 + 1) * ROW],
                                                    ACT.Identity, scale=trig_a[:, k.slot(), 0, j:j + 1])
                    last.then_inc(sc_scaled, 1)
                if a.within(NG):
                    act.wait_ge(red_done, (a + 1).n)
                    wait(act, triga_done, (a + -1).n)
                    nc.scalar.activation(redabs[:, a.slot(), :], red[:, a.slot(), :], ACT.Abs).then_inc(abs_done, 1)
                    nc.scalar.activation(trig[:, a.slot(), 1, :], red[:, a.slot(), :], ACT.Sin)
                    act.wait_ge(abs_done, (a + 1).n)
                    nc.scalar.activation(trig[:, a.slot(), 0, :], redabs[:, a.slot(), :], ACT.Sin,
                                         bias=half_pi[:, :], scale=-1.0).then_inc(trig_done, 1)
                s = k + -2
                if s.within(NG):
                    act.wait_ge(shift_done, (s + 1).n)
                    t = s.slot(UNROLL)
                    for j in range(G):
                        last = nc.scalar.activation(y_sb[:, t, j, :], y_sb[:, t, j, :], ACT.Identity,
                                                    bias=shift[:, t, j:j + 1], scale=rstd[:, t, j:j + 1])
                    last.then_inc(norm_done, 1)

            software_pipeline(act, -1, NG + 1, 2, NG - 2, node_step)

        @block.vector
        def _(dve):
            dve.wait_ge(consts, 16)
            s64, s32 = 1.0 / math.sqrt(NS), 1.0 / math.sqrt(MU)
            s96 = 1.0 / math.sqrt(NS + MU) / math.sqrt(NEIGHBORS)
            for w, s in ((fc_w2_sb, s64), (lin1_a_sb[0:NV, :], s32), (lin1_a_sb[NV:P, :], s64), (lin1_b_sb, s64), (sc_a_sb[0:NV, :], s32), (sc_a_sb[NV:P, :], s64), (sc_b_sb, s64),
                         (lin2_a_sb, s96), (lin2_b_sb, s96)):
                last = nc.vector.tensor_scalar(w[:, :], w[:, :], s, None, ALU.mult)
            last.then_inc(chain, 1)
            dve.wait_ge(chain, 1)
            nc.vector.tensor_scalar(lin2_a_sb[0:NS, NS:NS + 1], lin2_a_sb[0:NS, NS:NS + 1], 0.1, None, ALU.mult)
            nc.vector.tensor_scalar(lin2_b_sb[NV:P, :], lin2_b_sb[NV:P, :], 1.0 / math.sqrt(3.0), None,
                                    ALU.mult).then_inc(chain, 1)
            dve.wait_ge(chain, 2)
            nc.vector.tensor_scalar(lin2_b_sb[NV:P, ROW:ROWA], lin2_b_sb[NV:P, ROW:ROWA], 0.1, None,
                                    ALU.mult).then_inc(weights_scaled, 1)
            dve.wait_ge(idx_in, 32)
            nc.vector.tensor_copy(dst_f[:, :], dst_i[:, :]).then_inc(chain, 1)
            dve.wait_ge(chain, 3)
            dve.wait_ge(prep, 3)
            nc.vector.tensor_tensor(to_spare[:, :], spare_row[:, :], dst_f[:, :], ALU.subtract).then_inc(chain, 1)
            dve.wait_ge(chain, 4)

            def step(k):
                d = k + -3
                if d.within(NPAIR):
                    o = feat_sb[:, d.slot(UNROLL), :, :]
                    dve.wait_ge(out_copied, (d + 1).n)
                    nc.vector.tensor_tensor(
                        vq_sb[:, :, :, :],
                        o[:, :, ROWA:OUTW].rearrange("p j (c o) -> p j c o", o=1).to_broadcast([P, 2, MU, 3]),
                        q_sb[:, d.slot(UNROLL), :, 1:4].rearrange("p j (o c) -> p j o c", o=1).to_broadcast([P, 2, MU, 3]),
                        ALU.mult).then_inc(vq_done, 1)
                    wait(dve, dstrow_in[d.slot(UNROLL)], (d.round(UNROLL) + 1) * 16)
                    wait(dve, comb_ready, (d + -1).n)
                    for j in range(2):
                        last = nc.vector.tensor_scalar(same_sb[:, d.slot(), 2 * j:2 + j, :], dstrow_sb[:, d.slot(UNROLL), j:2, :],
                                                       dst_f[:, bass.ds(d.n * 2 + j, 1)], None, ALU.is_equal)
                    last.then_inc(same_done, 1)
                    dve.wait_ge(vq_done, (d + 1).n)
                    nc.vector.tensor_tensor(o[:, :, 0:NV], o[:, :, 0:NV],
                                            vq_sb[:, :, :, :].rearrange("p j c o -> p j (c o)"),
                                            ALU.add).then_inc(feat_done, 1)
                    dve.wait_ge(same_done, (d + 1).n)
                    for j in range(2):
                        last = nc.vector.tensor_tensor_reduce(
                            out=junk_sb[:, 2 * j:2 + j, :].rearrange("p b e -> p (b e)"),
                            in0=same_sb[:, d.slot(), 2 * j:2 + j, :].rearrange("p b e -> p (b e)"),
                            in1=later_sb[:, 0:(2 - j) * P], scale=1.0,
                            scalar=0.0, op0=ALU.mult, op1=ALU.add, accum_out=later_cnt[:, d.slot(), j:j + 1])
                    last.then_inc(cnt_done, 1)
                if d.within(NPAIR):
                    dve.wait_ge(cnt_done, (d + 1).n)
                    nc.vector.scalar_tensor_tensor(shift_sb[:, d.slot(), :], later_cnt[:, d.slot(), :], 1.0,
                                                   to_spare[:, bass.ds(d.n * 2, 2)], ALU.min, ALU.mult
                                                   ).then_inc(spare_done, 1)
                if k.within(NPAIR):
                    wait(dve, gathered[k.slot(UNROLL)], (k.round(UNROLL) + 1) * 32)
                    nc.vector.tensor_tensor(q_sb[:, k.slot(UNROLL), :, :], ea4_sb[:, bass.ds(k.n * 2, 2), :],
                                            x_sb[:, k.slot(UNROLL), 0:2 * ROWA:2 * ROWA - 1].rearrange(
                                                "p (j o) -> p j o", o=1).to_broadcast([P, 2, 4]),
                                            ALU.mult).then_inc(q_done, 1)
                if d.within(NPAIR):
                    dve.wait_ge(spare_done, (d + 1).n)
                    dve.wait_ge(comb_free, (d + 1).n)
                    nc.vector.tensor_tensor(row_sb[:, d.n % RING, :], shift_sb[:, d.slot(), :],
                                            dst_f[:, bass.ds(d.n * 2, 2)], ALU.add).then_inc(row_done, 1)
                if k.within(NPAIR):
                    f, q = f_sb[:, k.slot(), :, :], q_sb[:, k.slot(UNROLL), :, :]
                    w = W[:, :, 0:NW]
                    dve.wait_ge(q_done, (k + 1).n)
                    dve.wait_ge(f_copied, (k + 1).n)
                    nc.vector.tensor_tensor(tm_sb[:, :, :, :], f[:, :, NS:ROW].rearrange("p j (d c) -> p j d c", d=3),
                                            q[:, :, 1:4].rearrange("p j (d o) -> p j d o", o=1).to_broadcast([P, 2, 3, MU]),
                                            ALU.mult).then_inc(tm_done, 1)
                    dve.wait_ge(w_ready, (k + 1).n)
                    wait(dve, prodt_ready, (k + -1).n)
                    for j in range(2):
                        nc.vector.scalar_tensor_tensor(pa_sb[:, k.slot(), j, 0:NS], f[:, j, 0:NS], q[:, j, 0:1],
                                                       w[:, j, 0:NS], ALU.mult, ALU.mult)
                    dve.wait_ge(tm_done, (k + 1).n)
                    nc.vector.tensor_reduce(ts_sb[:, :, :], tm_sb[:, :, :, :].rearrange("p j d c -> p j c d"),
                                            mybir.AxisListType.X, ALU.add).then_inc(ts_done, 1)
                    for j in range(2):
                        nc.vector.scalar_tensor_tensor(
                            pb_sb[:, k.slot(), j, 0:NV].rearrange("p (d c) -> p d c", d=3),
                            f[:, j, NS:ROW].rearrange("p (d c) -> p d c", d=3), q[:, j, 0:1],
                            w[:, j, 2 * NS:2 * NS + MU].rearrange("p (o c) -> p o c", o=1).to_broadcast([P, 3, MU]),
                            ALU.mult, ALU.mult)
                    nc.vector.tensor_tensor(pa_sb[:, k.slot(), :, NS:P], f[:, :, 0:NS], w[:, :, NS:2 * NS], ALU.mult)
                    dve.wait_ge(ts_done, (k + 1).n)
                    nc.vector.tensor_tensor(pb_sb[:, k.slot(), :, NV:P], ts_sb[:, :, :], w[:, :, 2 * NS + MU:NW],
                                            ALU.mult).then_inc(prod_done, 1)

            software_pipeline(dve, 0, NPAIR + 2, 6, NPAIR - 1, step)

            C1 = 6.28125
            C2 = 2.0 * math.pi - C1
            MAGIC = 1.5 * 2.0 ** 23
            PI = 3.1415925
            LINKS = 5

            def angle(a):
                an, tu, t = ang[:, a.slot(), :], turns[:, a.slot(), :], a.slot(UNROLL)
                at = a.n * LINKS + 4
                wait(dve, acc_in[t], (a.round(UNROLL) + 1) * 16)
                wait(dve, xn_in[t], (a.round(UNROLL) + 1) * 16)
                nc.vector.tensor_tensor(an, cs_sb[:, t, :, ROW], xn_sb[:, t, :, 0], ALU.mult).then_inc(chain, 1)
                yield
                dve.wait_ge(chain, at + 1)
                nc.vector.tensor_scalar(tu, an, 1.0 / (2.0 * math.pi), MAGIC, ALU.mult, ALU.add).then_inc(chain, 1)
                yield
                dve.wait_ge(chain, at + 2)
                nc.vector.tensor_scalar(tu, tu, MAGIC, None, ALU.subtract).then_inc(chain, 1)
                yield
                for n, c in enumerate((C1, C2)):
                    dve.wait_ge(chain, at + 3 + n)
                    nc.vector.scalar_tensor_tensor(an, tu, -c, an, ALU.mult, ALU.add).then_inc(chain, 1)
                    yield
                dve.wait_ge(chain, at + LINKS)
                wait(dve, trig_done, (a + -1).n)
                nc.vector.tensor_scalar(red[:, a.slot(), :], an, -PI, PI, ALU.max, ALU.min).then_inc(red_done, 1)
                yield

            def scale_trig(b):
                dve.wait_ge(trig_done, (b + 1).n)
                attr = xn_sb[:, b.slot(UNROLL), :, 0:1].rearrange("p g o -> p o g")
                nc.vector.tensor_tensor(trig_a[:, b.slot(), :, :], trig[:, b.slot(), :, :],
                                        attr.to_broadcast([P, 2, G]), ALU.mult).then_inc(triga_done, 1)

            def variance_plus_eps(s):
                dve.wait_ge(mv_done, (s + 1).n)
                wait(dve, rstd_done, s.n)
                dve.sem_inc(dve_passed, 1)
                nc.vector.tensor_scalar(vareps[:, :], meanvar[:, s.slot(UNROLL), :, 1], EPS, None,
                                        ALU.add).then_inc(eps_done, 1)

            def layer_norm_shift(s):
                t = s.slot(UNROLL)
                dve.wait_ge(rstd_done, (s + 1).n)
                nc.vector.scalar_tensor_tensor(shift[:, t, :], meanvar[:, t, :, 0], -1.0, rstd[:, t, :],
                                               ALU.mult, ALU.mult).then_inc(shift_done, 1)

            def node_step(k):
                a = k + 2
                links = angle(a) if a.within(NG) else iter(())
                if k.within(NG):
                    t = k.slot(UNROLL)
                    ta = trig_a[:, k.slot(), :, :]
                    dve.wait_ge(triga_done, (k + 1).n)
                    dve.wait_ge(sc_ready, (k + 1).n)
                    wait(dve, stored[t], k.round(UNROLL) * 16)
                    for j in range(G // 2):
                        nc.vector.scalar_tensor_tensor(y_sb[:, t, j, :], sc_banks[k.slot()][j // 2][:, j % 2 * ROW:(j % 2 + 1) * ROW],
                                                       ta[:, 0, j:j + 1], xn_sb[:, t, j, 1:ROWA],
                                                       ALU.mult, ALU.add).then_inc(y_started, 1)
                        next(links, None)
                        if j == 0 and (k + -1).within(NG):
                            variance_plus_eps(k + -1)
                    if (k + 1).within(NG):
                        scale_trig(k + 1)
                    dve.wait_ge(y_started, (k + 1).n * (G // 2))
                    dve.wait_ge(sc_scaled, (k + 1).n)
                    dve.wait_ge(conv_scaled, (k + 1).n)
                    nc.vector.tensor_tensor(y_sb[:, t, :, :], y_sb[:, t, :, :], cs_sb[:, t, :, 0:ROW],
                                            ALU.add).then_inc(y_done, 1)
                    next(links, None)
                    dve.wait_ge(y_done, (k + 1).n)
                    for j in range(G):
                        last = nc.vector.bn_stats(stats[:, j, :], y_sb[:, t, j, :])
                        if j < G - 1:
                            next(links, None)
                    last.then_inc(stats_done, 1)
                    if (k + -1).within(NG):
                        layer_norm_shift(k + -1)
                    next(links, None)
                    dve.wait_ge(stats_done, (k + 1).n)
                    dve.sem_inc(dve_passed, 1)
                    for j in range(G):
                        last = nc.vector.bn_aggr(meanvar[:, t, j, :], stats[:, j, :])
                    last.then_inc(mv_done, 1)
                for _ in links:
                    pass
                if k.i is None and k.c == NG:
                    variance_plus_eps(k + -1)
                    layer_norm_shift(k + -1)
                if k.i is None and k.c == -1:
                    scale_trig(k + 1)
            software_pipeline(dve, -2, NG, UNROLL, NG - 3, node_step, each=2 * UNROLL)


def layouts(x, src, dst, edge_attr_4, edge_attr_8, node_vec1, sc_w0, sc_w1, lin1_w0, lin1_w1, fc_w1,
            fc_w2, lin2_w0, lin2_w1, lin3_w, tiles):
    n, e = x.shape[0], src.shape[0]
    rows = tiles * P
    f32 = np.float32
    xa = np.zeros((rows, ROWA), f32)
    xa[:n, 0], xa[:n, 1:1 + NV], xa[:n, 1 + NV:] = node_vec1[:, 0], x[:, NS:], x[:, :NS]
    src_p = np.zeros(rows, np.int32)
    src_p[:e] = src
    dst_p = np.full(rows, n, np.int32)
    dst_p[:e] = dst
    ea4 = np.zeros((rows, 4), f32)
    ea4[:e] = edge_attr_4
    ea8 = np.zeros((rows, EDGE_S), f32)
    ea8[:e] = edge_attr_8

    def by_component(w, rows_grouped, cols_grouped):
        u, c = w.shape
        m = np.zeros((u, 3, c, 3), f32)
        for d in range(3):
            m[:, d, :, d] = w
        if rows_grouped:
            m = m.transpose(1, 0, 2, 3).reshape(3 * u, c, 3)
        else:
            m = m.reshape(3 * u, c, 3)
        if cols_grouped:
            m = m.transpose(0, 2, 1)
        return np.ascontiguousarray(m.reshape(3 * u, 3 * c))

    lin2_a = np.zeros((P, NS + 1 + MU), f32)
    lin2_a[:NS, :NS] = lin2_w0[:NS]
    lin2_a[:NS, NS] = lin3_w[:NS, 0]
    lin2_a[NS:, NS + 1:] = lin2_w1[:NS]
    lin2_b = np.zeros((P, OUTW), f32)
    lin2_b[:NV, :NV] = by_component(lin2_w1[NS:], True, False)
    lin2_b[NV:, NV:ROW] = lin2_w0[NS:]
    lin2_b[NV:, ROW] = lin3_w[NS:, 0]
    sc_a = np.zeros((P, ROW), f32)
    sc_a[:NV, :NV] = by_component(sc_w1, False, False)
    sc_a[NV:, NV:] = sc_w0[:P - NV]
    lin1_a = np.zeros((P, ROW), f32)
    lin1_a[:NV, NS:] = by_component(lin1_w1, False, True)
    lin1_a[NV:, :NS] = lin1_w0[:P - NV]

    def two_tiles(w):
        m = np.zeros((2 * w.shape[0], 2 * w.shape[1]), f32)
        m[:w.shape[0], :w.shape[1]] = m[w.shape[0]:, w.shape[1]:] = w
        return m

    order = np.arange(P)
    values = {
        "fc_w1": two_tiles(fc_w1),
        "fc_w2": np.concatenate([fc_w2, fc_w2]),
        "lin1_a": lin1_a,
        "lin1_b": two_tiles(lin1_w0[P - NV:]),
        "lin2_a": lin2_a,
        "lin2_b": lin2_b,
        "sc_a": sc_a,
        "sc_b": np.concatenate([two_tiles(sc_w0[P - NV:])] * 2),
        "ident": np.eye(P, dtype=f32),
        "later": (np.arange(2 * P)[None, :] > order[:, None]).astype(f32),
    }
    constants = np.concatenate([np.pad(values[name], ((0, P - shape[0]), (0, 0)))
                                for name, shape in CONSTANTS.items()], axis=1)
    return {
        "xa": xa,
        "x_odd": np.concatenate([xa[:, 1 + P:], xa[:, 1:1 + P], xa[:, :1]], axis=1),
        "x_last": np.ascontiguousarray(xa[:, 1 + P:].reshape(tiles // G, P, G * (ROW - P))),
        "src": np.ascontiguousarray(src_p.reshape(P, tiles // 2, 2).transpose(1, 0, 2)),
        "dst": dst_p.reshape(P, tiles),
        "dst_rows": np.ascontiguousarray(dst_p.reshape(P, tiles).T).reshape(tiles // 2, 2, P),
        "ea4": ea4.reshape(P, tiles, 4),
        "ea8t": np.ascontiguousarray(ea8.reshape(P, tiles // 2, 2, EDGE_S).transpose(1, 2, 3, 0)
                                     ).reshape(tiles // 2, 2 * EDGE_S, P),
        "constants": constants,
    }


def kernel(x, src, dst, edge_attr_4, edge_attr_8, node_vec1, L0_gnn_sc_w0, L0_gnn_sc_w1, L0_gnn_lin1_w0,
           L0_gnn_lin1_w1, L0_gnn_fc_w1, L0_gnn_fc_w2, L0_gnn_lin2_w0, L0_gnn_lin2_w1, L0_gnn_lin3_w):
    import concourse.bacc as bacc
    from concourse.bass_utils import run_bass_kernel_spmd

    n = x.shape[0]
    tiles = -(-max(n + 1, src.shape[0]) // (P * 2 * G)) * 2 * G
    arrays = layouts(*(np.asarray(a) for a in (
        x, src, dst, edge_attr_4, edge_attr_8, node_vec1, L0_gnn_sc_w0, L0_gnn_sc_w1, L0_gnn_lin1_w0,
        L0_gnn_lin1_w1, L0_gnn_fc_w1, L0_gnn_fc_w2, L0_gnn_lin2_w0, L0_gnn_lin2_w1, L0_gnn_lin3_w)), tiles)
    nc = bacc.Bacc("TRN2", target_bir_lowering=False, num_devices=1)
    args = {k: nc.dram_tensor(k, a.shape, mybir.dt.from_np(a.dtype), kind="ExternalInput").ap()
            for k, a in arrays.items()}
    args["acc"] = nc.dram_tensor("acc", [(tiles + SPARE) * P, ROWA], mybir.dt.float32, kind="Internal").ap()
    args["out"] = nc.dram_tensor("out", [tiles * P, ROW], mybir.dt.float32, kind="ExternalOutput").ap()
    gnn_program(nc, **args)
    r = run_bass_kernel_spmd(nc, [arrays], core_ids=[0])
    got = r.results[0]["out"][:n]
    return np.concatenate([got[:, NV:], got[:, :NV]], axis=1)
```
